# Optimizing a Trainium2 kernel written in Bass

```python
import numpy as np
import jax
import jax.numpy as jnp

def _softmax(x, axis=-1):
    return jax.nn.softmax(x, axis=axis)

def _gelu(x):
    return jax.nn.gelu(x, approximate=True)

def _silu(x):
    return jax.nn.silu(x)

def _sigmoid(x):
    return jax.nn.sigmoid(x)

def _layernorm(x, axis=-1, eps=1e-05):
    m = jnp.mean(x, axis=axis, keepdims=True)
    v = jnp.var(x, axis=axis, keepdims=True)
    return (x - m) / jnp.sqrt(v + eps)

def _scatter_add(tgt, idx, src, axis=0):
    return tgt.at[idx].add(src)

def _segment_sum(src, seg, n):
    return jax.ops.segment_sum(src, seg, n)
kernel_name = 'mk_adj_preln_d1_adj_r2_4a29fc'

def setup_inputs(seed: int=0):
    np.random.seed(seed)
    _w = jnp.asarray

    def _rec_inputs():
        import jax
        import jax.numpy as jnp
        _gk = jax.random.key(seed)
        x = -0.0001538 + 1 * jax.random.normal(jax.random.fold_in(_gk, 1), (64, 128, 384), jnp.float32)
        _a = jax.random.bernoulli(jax.random.fold_in(_gk, 2), 0.015625, (64, 128, 128))
        _a = jnp.logical_or(_a, jnp.eye(128, dtype=bool))
        adj = _a
        return (x, adj)
    x, adj = _rec_inputs()

    def _L0_gnn_setup():
        import jax, jax.numpy as jnp
        import numpy as np
        B, S, H = (4, 1024, 384)
        NUM_HEADS = 6
        HEAD_SIZE = H // NUM_HEADS
        NEG = -9000000000000000.0

        def _heads(x):
            b, s, _ = x.shape
            return x.reshape(b, s, NUM_HEADS, HEAD_SIZE).transpose(0, 2, 1, 3)
        key = jax.random.key(seed)
        ks = jax.random.split(key, 10)
        seq_inputs = jax.random.normal(ks[0], (B, S, H), dtype=jnp.float32)
        gm = jax.random.randint(ks[1], (B, S, S), 0, 2) > 0
        graph_mask = gm | jnp.eye(S, dtype=bool)[None]
        sc = 1.0 / np.sqrt(H)
        Wq = jax.random.normal(ks[2], (H, H), dtype=jnp.float32) * sc
        bq = jnp.zeros((H,), dtype=jnp.float32)
        Wk = jax.random.normal(ks[3], (H, H), dtype=jnp.float32) * sc
        bk = jnp.zeros((H,), dtype=jnp.float32)
        Wv = jax.random.normal(ks[4], (H, H), dtype=jnp.float32) * sc
        bv = jnp.zeros((H,), dtype=jnp.float32)
        Wf = jax.random.normal(ks[5], (H, H), dtype=jnp.float32) * sc
        bf = jnp.zeros((H,), dtype=jnp.float32)
        return {'seq_inputs': seq_inputs, 'Wq': Wq, 'bq': bq, 'Wk': Wk, 'bk': bk, 'Wv': Wv, 'bv': bv, 'Wf': Wf, 'bf': bf, 'graph_mask': graph_mask}
    _L0_gnn_all = _L0_gnn_setup()
    _L0_gnn_in = {k: v for k, v in _L0_gnn_all.items() if k in ('Wq', 'bq', 'Wk', 'bk', 'Wv', 'bv', 'Wf', 'bf')}
    del _L0_gnn_all
    return {'x': x, 'adj': adj, 'L0_gnn_Wq': _L0_gnn_in['Wq'], 'L0_gnn_bq': _L0_gnn_in['bq'], 'L0_gnn_Wk': _L0_gnn_in['Wk'], 'L0_gnn_bk': _L0_gnn_in['bk'], 'L0_gnn_Wv': _L0_gnn_in['Wv'], 'L0_gnn_bv': _L0_gnn_in['bv'], 'L0_gnn_Wf': _L0_gnn_in['Wf'], 'L0_gnn_bf': _L0_gnn_in['bf']}

def reference(x, adj, L0_gnn_Wq, L0_gnn_bq, L0_gnn_Wk, L0_gnn_bk, L0_gnn_Wv, L0_gnn_bv, L0_gnn_Wf, L0_gnn_bf):
    import jax
    import jax.numpy as jnp

    def _L0_gnn_ref(seq_inputs, Wq, bq, Wk, bk, Wv, bv, Wf, bf, graph_mask):
        import jax, jax.numpy as jnp
        import numpy as np
        B, S, H = (4, 1024, 384)
        NUM_HEADS = 6
        HEAD_SIZE = H // NUM_HEADS
        NEG = -9000000000000000.0

        def _heads(x):
            b, s, _ = x.shape
            return x.reshape(b, s, NUM_HEADS, HEAD_SIZE).transpose(0, 2, 1, 3)
        q = _heads(seq_inputs @ Wq + bq)
        k = _heads(seq_inputs @ Wk + bk)
        v = _heads(seq_inputs @ Wv + bv)
        scores = jnp.einsum('bhqd,bhkd->bhqk', q, k) / np.sqrt(HEAD_SIZE)
        bias = jnp.where(graph_mask, 0.0, NEG)[:, None]
        probs = jax.nn.softmax(scores + bias, axis=-1)
        ctx = jnp.einsum('bhqk,bhkd->bhqd', probs, v)
        ctx = ctx.transpose(0, 2, 1, 3).reshape(seq_inputs.shape[0], seq_inputs.shape[1], H)
        return ctx @ Wf + bf
    h = jnp.maximum(_layernorm(x, axis=-1), 0.0)
    x = x + _L0_gnn_ref(h, L0_gnn_Wq, L0_gnn_bq, L0_gnn_Wk, L0_gnn_bk, L0_gnn_Wv, L0_gnn_bv, L0_gnn_Wf, L0_gnn_bf, adj)
    return x

_drawn_inputs = setup_inputs


def setup_inputs(seed=0):
    import zlib

    import numpy as np

    out = dict(_drawn_inputs(seed))
    spreads = {'L0_gnn_bq': (0.0, 0.672),
     'L0_gnn_bk': (0.0, 0.8),
     'L0_gnn_bv': (0.0, 0.1),
     'L0_gnn_bf': (0.0, 0.1)}
    factors = {}
    for name, (base, spread) in spreads.items():
        noise = np.random.default_rng([zlib.crc32(name.encode()), seed]).standard_normal(out[name].shape)
        drawn = base * np.exp(spread * noise) if base else spread * noise
        out[name] = jnp.asarray(drawn.astype(out[name].dtype))
    for name, factor in factors.items():
        out[name] = (out[name] * factor).astype(out[name].dtype)
    return out
```

```python
from contextlib import ExitStack

import concourse.bass as bass
from concourse import mybir

ALU = mybir.AluOpType
ACT = mybir.ActivationFunctionType
AX = mybir.AxisListType
F32 = mybir.dt.float32
F32R = mybir.dt.float32r
F16 = mybir.dt.float16
I32 = mybir.dt.int32
U8 = mybir.dt.uint8

P = 128
GRAPHS, N, H = 64, 128, 384
HEADS, D = 6, 64
C = H // P
B = 4
GROUPS = GRAPHS // B
HALVES = 2
K = HEADS // HALVES
T = B * HALVES
QK = 2 * C
EPS = 1e-5
NEG = -9000000000000000.0
SCALE = float(D) ** -0.5
TINY = 2.0 ** -100
EXPONENT_BITS = 0x7F800000

FIRST = (-2, -1, 0)
REPS = (GROUPS - 4) // 2
LAST = (GROUPS - 3, GROUPS - 2, GROUPS - 1)

FILL = {0: [("qk", 0)], 1: [("v", 0)], 2: [("qk", 1)], 3: [("v", 1)], 4: [("qk", 2)], 5: [("v", 2)],
        6: [("qk", 3)], 7: [("qk", 4)], 8: [("qk", 5)], 9: [("v", 3)]}
FILL_LATE = {5: [("ht", 0)], 6: [("ht", 1)], 7: [("ht", 2)], 8: [("ht", 3)]}
SLOTS = T + 2
BANK_USES = [("qk", 0), ("v", 0), ("qk", 1), ("v", 1), ("f", 0), ("qk", 2), ("v", 2), ("f", 1), ("ht", 0),
             ("qk", 3), ("ht", 1), ("qk", 4), ("f", 2), ("ht", 2), ("qk", 5), ("ht", 3), ("v", 3), ("f", 3)]
BANK = {use: n % 2 for n, use in enumerate(BANK_USES)}


def nth(per_group, group, item, i):
    return per_group * group + item + 1 + 2 * per_group * i


def loads(group, i):
    return 16 * (group // 2 + 1) + 16 * i


def attends(g):
    return 0 <= g < GROUPS


def projects(g):
    return 0 <= g + 1 < GROUPS


def norms(g):
    return 0 <= g + 2 < GROUPS


def build(nc, x, adj, wq, bq, wk, bk, wv, bv, wf, bf, out):
    x_v = x.rearrange("(g b) p h -> g p b h", b=B)
    adj_v = adj.rearrange("(g b) p k -> g p b k", b=B)
    out_v = out.rearrange("(g b) p h -> g p b h", b=B)

    ctx = ExitStack()
    with ctx:
        def sb(name, shape, dt=F32):
            return ctx.enter_context(nc.sbuf_tensor(name, shape, dt))

        def pb(name):
            return ctx.enter_context(nc.psum_tensor(name, [P, 512], F32))

        def sem(name):
            return ctx.enter_context(nc.semaphore(name))

        w_raw = [sb(f"w_raw{n}", [P, C, H]) for n in range(4)]
        w_hi = [sb(f"w_hi{n}", [P, C, H], F32R) for n in range(4)]
        w_lo = [sb(f"w_lo{n}", [P, C, H], F32R) for n in range(4)]
        bias_raw = sb("bias_raw", [P, 3, C])
        bias_qk = sb("bias_qk", [P, QK])
        bv_cols = sb("bv_cols", [P, C, P])
        bf_rows = sb("bf_rows", [P, H])
        b_out = sb("b_out", [P, H])
        wv_most = sb("wv_most", [P, 1])
        wv_most_all = sb("wv_most_all", [P, 1])
        wv_bound = sb("wv_bound", [P, 1])
        v_scale = sb("v_scale", [P, 1])
        v_unscale = sb("v_unscale", [P, 1])
        ident = sb("ident", [P, P])
        minus_half = sb("minus_half", [P, B])
        eps = sb("eps", [P, B])
        x_sb = [sb(f"x_sb{n}", [P, B, H]) for n in range(2)]
        x_bf = [sb(f"x_bf{n}", [P, B, H]) for n in range(2)]
        adj_sb = [sb(f"adj_sb{n}", [P, B, N], U8) for n in range(2)]
        mask = [sb(f"mask{n}", [P, B, N]) for n in range(2)]
        ht_hi = [sb(f"ht_hi{n}", [P, C, B * N], F32R) for n in range(2)]
        ht_lo = [sb(f"ht_lo{n}", [P, C, B * N], F32R) for n in range(2)]
        qkt = [sb(f"qkt{n}", [P, QK, B * N]) for n in range(2)]
        v_hi = [sb(f"v_hi{n}", [P, B, H], F16) for n in range(2)]
        v_lo = [sb(f"v_lo{n}", [P, B, H], F16) for n in range(2)]
        stats = sb("stats", [P, B, 6])
        moments = sb("moments", [P, B, 2])
        var_eps = sb("var_eps", [P, B])
        rstd = sb("rstd", [P, B])
        h_sb = sb("h_sb", [P, B, H])
        masked = [sb(f"masked{n}", [P, K, N]) for n in range(2)]
        neg_max = [sb(f"neg_max{n}", [P, K]) for n in range(2)]
        probs = [sb(f"probs{n}", [P, K, N]) for n in range(2)]
        pt_hi = [sb(f"pt_hi{n}", [P, K * N], F16) for n in range(2)]
        pt_lo = [sb(f"pt_lo{n}", [P, K * N], F16) for n in range(2)]
        sums = [sb(f"sums{n}", [P, HEADS]) for n in range(2)]
        inv_sums = [sb(f"inv_sums{n}", [P, HEADS]) for n in range(2)]
        ctx_sb = [sb(f"ctx_sb{n}", [P, H]) for n in range(2)]
        ct_hi = [sb(f"ct_hi{n}", [P, H], F32R) for n in range(2)]
        ct_lo = [sb(f"ct_lo{n}", [P, H], F32R) for n in range(2)]
        y_sb = [sb(f"y_sb{n}", [P, H]) for n in range(2)]

        ps_proj = [pb(f"ps_proj{n}") for n in range(2)]
        ps_scores = [pb(f"ps_scores{n}") for n in range(2)]
        ps_pt = [pb(f"ps_pt{n}") for n in range(2)]
        ps_ctx = pb("ps_ctx")
        ps_ct = pb("ps_ct")

        x_loaded = [sem(f"x_loaded{n}") for n in range(2)]
        adj_loaded = [sem(f"adj_loaded{n}") for n in range(2)]
        w_loaded = [sem(f"w_loaded{n}") for n in range(4)]
        bias_loaded = sem("bias_loaded")
        bf_loaded = sem("bf_loaded")
        y_stored = [sem(f"y_stored{n}") for n in range(2)]
        consts_set = sem("consts_set")
        wv_reduced = sem("wv_reduced")
        wv_reduced_all = sem("wv_reduced_all")
        v_scale_step = sem("v_scale_step")
        w_scaled = sem("w_scaled")
        w_hi_ready = sem("w_hi_ready")
        w_split = sem("w_split")
        biases_ready = sem("biases_ready")
        bv_projected = sem("bv_projected")
        b_out_ready = sem("b_out_ready")
        stats_ready = sem("stats_ready")
        moments_ready = sem("moments_ready")
        var_eps_ready = sem("var_eps_ready")
        rstd_ready = sem("rstd_ready")
        h_ready = sem("h_ready")
        x_bf_ready = sem("x_bf_ready")
        mask_ready = sem("mask_ready")
        h_transposed = sem("h_transposed")
        ht_hi_ready = sem("ht_hi_ready")
        ht_split = sem("ht_split")
        qk_projected = sem("qk_projected")
        qk_stored = sem("qk_stored")
        v_projected = sem("v_projected")
        v_hi_ready = sem("v_hi_ready")
        v_split = sem("v_split")
        scores_ready = sem("scores_ready")
        scores_masked = sem("scores_masked")
        max_ready = sem("max_ready")
        probs_ready = sem("probs_ready")
        probs_transposed = sem("probs_transposed")
        pt_hi_ready = sem("pt_hi_ready")
        pt_split = sem("pt_split")
        values_weighted = sem("values_weighted")
        sums_inverted = sem("sums_inverted")
        ctx_normalized = sem("ctx_normalized")
        ctx_transposed = sem("ctx_transposed")
        ct_hi_ready = sem("ct_hi_ready")
        ct_split = sem("ct_split")
        y_projected = sem("y_projected")
        y_ready = sem("y_ready")

        block = ctx.enter_context(nc.Block())

        @block.sync
        def _(sp):
            def load(group, i):
                par = group % 2
                if group >= 2:
                    sp.wait_ge(h_ready, nth(B, group - 2, B - 1, i))
                    sp.wait_ge(x_bf_ready, nth(1, group - 2, 0, i))
                    sp.wait_ge(mask_ready, nth(1, group - 2, 0, i))
                at = group + 2 * i
                sp.dma_start(x_sb[par][:], x_v[at, :, :, :]).then_inc(x_loaded[par], 16)
                sp.dma_start(adj_sb[par][:], adj_v[at, :, :, :]).then_inc(adj_loaded[par], 16)

            def step(g, i):
                if g + 3 < GROUPS:
                    load(g + 3, i)
                if attends(g):
                    for b in range(B):
                        sp.wait_ge(y_ready, nth(B, g, b, i))
                        sp.dma_start(out_v[g + 2 * i, :, b, :], y_sb[b % 2][:]).then_inc(y_stored[b % 2], 16)

            load(0, 0)
            for n, w in enumerate((wq, wk, wv, wf)):
                sp.dma_start(w_raw[n][:], w.rearrange("(c p) n -> p c n", p=P)).then_inc(w_loaded[n], 16)
            for g in FIRST:
                step(g, 0)
            with sp.Fori(0, REPS) as i:
                step(1, i)
                step(2, i)
            for g in LAST:
                step(g, 0)
            for n in range(2):
                sp.wait_ge(y_stored[n], 16 * GRAPHS // 2)

        @block.gpsimd
        def _(pool):
            def inverse_deviation(group, i):
                pool.wait_ge(moments_ready, nth(1, group, 0, i))
                nc.gpsimd.tensor_tensor(var_eps[:], moments[:, :, 1], eps[:], ALU.add).then_inc(var_eps_ready, 1)
                pool.wait_ge(var_eps_ready, nth(1, group, 0, i))
                if group >= 1:
                    pool.wait_ge(h_ready, nth(B, group - 1, B - 1, i))
                nc.gpsimd.tensor_tensor(rstd[:], var_eps[:], minus_half[:], ALU.pow).then_inc(rstd_ready, 1)

            def residual(group, i):
                par = group % 2
                pool.wait_ge(x_loaded[par], loads(group, i))
                if group >= 2:
                    pool.wait_ge(y_ready, nth(B, group - 2, B - 1, i))
                nc.gpsimd.tensor_tensor(x_bf[par][:], x_sb[par][:],
                                        b_out[:].unsqueeze(1).broadcast_to([P, B, H]), ALU.add)\
                    .then_inc(x_bf_ready, 1)

            def step(g, i):
                if norms(g):
                    inverse_deviation(g + 2, i)
                if projects(g):
                    residual(g + 1, i)

            nc.gpsimd.memset(minus_half[:], -0.5).then_inc(consts_set, 1)
            nc.gpsimd.memset(eps[:], EPS).then_inc(consts_set, 1)
            nc.gpsimd.memset(ident[:], 0.0).then_inc(consts_set, 1)
            pool.wait_ge(consts_set, 3)
            nc.gpsimd.affine_select(out=ident[:], in_=ident[:], compare_op=ALU.not_equal, fill=1.0, base=0,
                                    pattern=[[-1, P]], channel_multiplier=1).then_inc(consts_set, 1)
            step(FIRST[0], 0)
            pool.wait_ge(wv_reduced, 1)
            nc.gpsimd.partition_all_reduce(wv_most_all[:], wv_most[:], P, bass.bass_isa.ReduceOp.max)\
                .then_inc(wv_reduced_all, 1)
            pool.wait_ge(b_out_ready, 1)
            for g in FIRST[1:]:
                step(g, 0)
            with pool.Fori(0, REPS) as i:
                step(1, i)
                step(2, i)
            for g in LAST:
                step(g, 0)

        @block.scalar
        def _(act):
            def exponentials(g, t, i):
                b, half = divmod(t, HALVES)
                act.wait_ge(max_ready, nth(T, g, t, i))
                if g >= 1 or t >= 2:
                    act.wait_ge(probs_transposed, nth(T, g, t - 2, i))
                if g >= 1 or b >= 2:
                    act.wait_ge(sums_inverted, nth(B, g, b - 2, i))
                for k in range(K):
                    head = HALVES * k + half
                    last = nc.scalar.activation(probs[t % 2][:, k, :], masked[t % 2][:, k, :], ACT.Exp,
                                                bias=neg_max[t % 2][:, k:k + 1],
                                                accum_out=sums[b % 2][:, head:head + 1])
                last.then_inc(probs_ready, 1)

            def probs_hi(g, t, i):
                act.wait_ge(probs_transposed, nth(T, g, t, i))
                if g >= 1 or t >= 2:
                    act.wait_ge(values_weighted, nth(T, g, t - 2, i))
                nc.scalar.activation(pt_hi[t % 2][:], ps_pt[t % 2][:, 0:K * N], ACT.Copy).then_inc(pt_hi_ready, 1)

            def ctx_hi(g, b, i):
                act.wait_ge(ctx_transposed, nth(B, g, b, i))
                if g >= 1 or b >= 2:
                    act.wait_ge(y_projected, nth(B, g, b - 2, i))
                nc.scalar.activation(ct_hi[b % 2][:], ps_ct[:, 0:H], ACT.Copy).then_inc(ct_hi_ready, 1)

            def store_qk(group, j, i):
                act.wait_ge(qk_projected, nth(QK, group, j, i))
                if group == 0 and j == 0:
                    act.wait_ge(biases_ready, 1)
                if group >= 2 and j == 0:
                    act.wait_ge(scores_ready, nth(T, group - 2, T - 1, i))
                nc.scalar.activation(qkt[group % 2][:, j, :], ps_proj[BANK["qk", j]][:], ACT.Identity,
                                     bias=bias_qk[:, j:j + 1], scale=SCALE if j < C else 1.0)\
                    .then_inc(qk_stored, 1)

            def values_hi(group, b, i):
                act.wait_ge(v_projected, nth(B, group, b, i))
                if group >= 2 and b == 0:
                    act.wait_ge(values_weighted, nth(T, group - 2, T - 1, i))
                nc.scalar.activation(v_hi[group % 2][:, b, :], ps_proj[BANK["v", b]][:, 0:H], ACT.Copy)\
                    .then_inc(v_hi_ready, 1)

            def normed_hi(group, b, i):
                act.wait_ge(h_transposed, nth(B, group, b, i))
                if group >= 2 and b == 0:
                    act.wait_ge(qk_projected, nth(QK, group - 2, QK - 1, i))
                    act.wait_ge(v_projected, nth(B, group - 2, B - 1, i))
                nc.scalar.activation(ht_hi[group % 2][:, :, b * N:(b + 1) * N],
                                     ps_proj[BANK["ht", b]][:, 0:H].rearrange("p (c n) -> p c n", c=C),
                                     ACT.Relu).then_inc(ht_hi_ready, 1)

            def fill(g, uses, i):
                for kind, j in uses:
                    if kind == "qk" and projects(g):
                        store_qk(g + 1, j, i)
                    if kind == "v" and projects(g):
                        values_hi(g + 1, j, i)
                    if kind == "ht" and norms(g):
                        normed_hi(g + 2, j, i)

            def step(g, i):
                for n in range(SLOTS):
                    if attends(g):
                        if 1 <= n <= T:
                            probs_hi(g, n - 1, i)
                        if n % 2 and n >= 3:
                            ctx_hi(g, (n - 3) // 2, i)
                        if n < T:
                            exponentials(g, n, i)
                    fill(g, FILL[n], i)
                    fill(g, FILL_LATE.get(n, []), i)

            act.dma_start(bias_raw[:, 0, :], bq.rearrange("(c p) -> p c", p=P), allow_slow_non_contiguous=True)\
                .then_inc(bias_loaded, 16)
            act.dma_start(bias_raw[:, 1, :], bk.rearrange("(c p) -> p c", p=P), allow_slow_non_contiguous=True)\
                .then_inc(bias_loaded, 16)
            act.dma_start(bias_raw[:, 2, :], bv.rearrange("(c p) -> p c", p=P), allow_slow_non_contiguous=True)\
                .then_inc(bias_loaded, 16)
            act.dma_start(bf_rows[:], bf.partition_broadcast(P)).then_inc(bf_loaded, 16)
            step(FIRST[0], 0)
            for n in range(4):
                act.wait_ge(w_loaded[n], 16)
                if n >= 2:
                    act.wait_ge(w_scaled, n - 1)
                nc.scalar.activation(w_hi[n][:], w_raw[n][:], ACT.Copy).then_inc(w_hi_ready, 1)
            for g in FIRST[1:]:
                step(g, 0)
            with act.Fori(0, REPS) as i:
                step(1, i)
                step(2, i)
            for g in LAST:
                step(g, 0)

        @block.vector
        def _(dve):
            def statistics(group, i):
                dve.wait_ge(x_loaded[group % 2], loads(group, i))
                if group >= 1:
                    dve.wait_ge(moments_ready, nth(1, group - 1, 0, i))
                for b in range(B):
                    last = nc.vector.bn_stats(stats[:, b, :], x_sb[group % 2][:, b, :])
                last.then_inc(stats_ready, 1)

            def additive_mask(group, i):
                dve.wait_ge(adj_loaded[group % 2], loads(group, i))
                if group >= 2:
                    dve.wait_ge(scores_masked, nth(T, group - 2, T - 1, i))
                nc.vector.tensor_scalar(mask[group % 2][:], adj_sb[group % 2][:], -NEG, NEG, ALU.mult, ALU.add)\
                    .then_inc(mask_ready, 1)

            def wait_to_aggregate(group, i):
                dve.wait_ge(stats_ready, nth(1, group, 0, i))
                if group >= 1:
                    dve.wait_ge(h_ready, nth(B, group - 1, B - 1, i))
                    dve.wait_ge(var_eps_ready, nth(1, group - 1, 0, i))

            def aggregate(group):
                for b in range(B):
                    last = nc.vector.bn_aggr(moments[:, b, :], stats[:, b, :])
                last.then_inc(moments_ready, 1)

            def normalize(group, b, i):
                dve.wait_ge(rstd_ready, nth(1, group, 0, i))
                if group >= 1:
                    dve.wait_ge(h_transposed, nth(B, group - 1, b, i))
                nc.vector.tensor_scalar(h_sb[:, b, :], x_sb[group % 2][:, b, :], moments[:, b, 0:1],
                                        rstd[:, b:b + 1], ALU.subtract, ALU.mult).then_inc(h_ready, 1)

            def mask_and_max(g, t, i):
                dve.wait_ge(scores_ready, nth(T, g, t, i))
                dve.wait_ge(mask_ready, nth(1, g, 0, i))
                if g >= 1 or t >= 2:
                    dve.wait_ge(probs_ready, nth(T, g, t - 2, i))
                nc.vector.tensor_tensor(masked[t % 2][:],
                                        ps_scores[t % 2][:, 0:K * N].rearrange("p (k n) -> p k n", k=K),
                                        mask[g % 2][:, t // HALVES, :].unsqueeze(1).broadcast_to([P, K, N]),
                                        ALU.add).then_inc(scores_masked, 1)
                dve.wait_ge(scores_masked, nth(T, g, t, i))
                nc.vector.tensor_reduce(neg_max[t % 2][:], masked[t % 2][:], AX.X, ALU.max, negate=True)\
                    .then_inc(max_ready, 1)

            def probs_lo(g, t, i):
                dve.wait_ge(pt_hi_ready, nth(T, g, t, i))
                nc.vector.tensor_tensor(pt_lo[t % 2][:], ps_pt[t % 2][:, 0:K * N], pt_hi[t % 2][:], ALU.subtract)\
                    .then_inc(pt_split, 1)

            def normalize_ctx(g, b, i):
                dve.wait_ge(probs_ready, nth(T, g, HALVES * b + 1, i))
                if g >= 1 or b >= 2:
                    dve.wait_ge(ctx_normalized, nth(B, g, b - 2, i))
                nc.vector.reciprocal(inv_sums[b % 2][:], sums[b % 2][:]).then_inc(sums_inverted, 1)
                dve.wait_ge(sums_inverted, nth(B, g, b, i))
                dve.wait_ge(values_weighted, nth(T, g, HALVES * b + 1, i))
                if g >= 1 or b >= 2:
                    dve.wait_ge(ctx_transposed, nth(B, g, b - 2, i))
                nc.vector.tensor_tensor(ctx_sb[b % 2][:].rearrange("p (h d) -> p h d", h=HEADS),
                                        ps_ctx[:, 0:H].rearrange("p (h d) -> p h d", h=HEADS),
                                        inv_sums[b % 2][:].unsqueeze(2).broadcast_to([P, HEADS, D]),
                                        ALU.mult).then_inc(ctx_normalized, 1)

            def ctx_lo(g, b, i):
                dve.wait_ge(ct_hi_ready, nth(B, g, b, i))
                nc.vector.tensor_tensor(ct_lo[b % 2][:], ps_ct[:, 0:H], ct_hi[b % 2][:].bitcast(F32), ALU.subtract)\
                    .then_inc(ct_split, 1)

            def finish(g, b, i):
                dve.wait_ge(y_projected, nth(B, g, b, i))
                dve.wait_ge(x_bf_ready, nth(1, g, 0, i))
                if g >= 1 or b >= 2:
                    dve.wait_ge(y_stored[b % 2], 16 * (2 * g + b // 2) + 64 * i)
                nc.vector.tensor_tensor(y_sb[b % 2][:], ps_proj[BANK["f", b]][:, 0:H], x_bf[g % 2][:, b, :],
                                        ALU.add).then_inc(y_ready, 1)

            def values_lo(group, b, i):
                dve.wait_ge(v_hi_ready, nth(B, group, b, i))
                nc.vector.tensor_tensor(v_lo[group % 2][:, b, :], ps_proj[BANK["v", b]][:, 0:H],
                                        v_hi[group % 2][:, b, :], ALU.subtract).then_inc(v_split, 1)

            def normed_lo(group, b, i):
                dve.wait_ge(ht_hi_ready, nth(B, group, b, i))
                at = slice(b * N, (b + 1) * N)
                nc.vector.scalar_tensor_tensor(out=ht_lo[group % 2][:, :, at],
                                               in0=ps_proj[BANK["ht", b]][:, 0:H].rearrange("p (c n) -> p c n", c=C),
                                               scalar=0.0, in1=ht_hi[group % 2][:, :, at].bitcast(F32),
                                               op0=ALU.max, op1=ALU.subtract).then_inc(ht_split, 1)

            def fill(g, uses, i):
                for kind, j in uses:
                    if kind == "v" and projects(g):
                        values_lo(g + 1, j, i)
                    if kind == "ht" and norms(g):
                        normed_lo(g + 2, j, i)

            def step(g, i):
                for n in range(SLOTS):
                    if attends(g) and n < T:
                        mask_and_max(g, n, i)
                    if n == 0:
                        if norms(g):
                            statistics(g + 2, i)
                            wait_to_aggregate(g + 2, i)
                        if projects(g):
                            additive_mask(g + 1, i)
                        if norms(g):
                            aggregate(g + 2)
                    if attends(g):
                        if 1 <= n <= T:
                            probs_lo(g, n - 1, i)
                        if n % 2 and n >= 3:
                            ctx_lo(g, (n - 3) // 2, i)
                    fill(g, FILL[n], i)
                    if norms(g) and 3 <= n < 3 + B:
                        normalize(g + 2, n - 3, i)
                    if attends(g):
                        if n % 2 == 0 and n >= 2:
                            normalize_ctx(g, (n - 2) // 2, i)
                        if n % 2 and n >= 3:
                            finish(g, (n - 3) // 2, i)
                    fill(g, FILL_LATE.get(n, []), i)

            def split(n):
                dve.wait_ge(w_hi_ready, n + 1)
                nc.vector.tensor_tensor(w_lo[n][:], w_raw[n][:], w_hi[n][:].bitcast(F32), ALU.subtract)\
                    .then_inc(w_split, 1)

            step(FIRST[0], 0)
            dve.wait_ge(w_loaded[2], 16)
            nc.vector.tensor_reduce(wv_most[:], w_raw[2][:], AX.XY, ALU.max, apply_absolute_value=True)\
                .then_inc(wv_reduced, 1)
            split(0)
            split(1)
            dve.wait_ge(wv_reduced_all, 1)
            nc.vector.tensor_scalar(wv_bound[:], wv_most_all[:], TINY, None, ALU.max).then_inc(v_scale_step, 1)
            dve.wait_ge(v_scale_step, 1)
            nc.vector.tensor_scalar(v_scale[:].bitcast(I32), wv_bound[:].bitcast(I32), EXPONENT_BITS, None,
                                    ALU.bitwise_and).then_inc(v_scale_step, 1)
            dve.wait_ge(v_scale_step, 2)
            nc.vector.reciprocal(v_unscale[:], v_scale[:]).then_inc(v_scale_step, 1)
            dve.wait_ge(v_scale_step, 3)
            nc.vector.tensor_scalar(w_raw[2][:], w_raw[2][:], v_unscale[:, 0:1], None, ALU.mult).then_inc(w_scaled, 1)
            dve.wait_ge(w_loaded[3], 16)
            nc.vector.tensor_scalar(w_raw[3][:], w_raw[3][:], v_scale[:, 0:1], None, ALU.mult).then_inc(w_scaled, 1)
            dve.wait_ge(bias_loaded, 48)
            nc.vector.tensor_scalar(bias_qk[:, 0:C], bias_raw[:, 0, :], SCALE, None, ALU.mult)
            nc.vector.tensor_copy(bias_qk[:, C:QK], bias_raw[:, 1, :]).then_inc(biases_ready, 1)
            nc.vector.tensor_scalar(bv_cols[:], bias_raw[:, 2, :].unsqueeze(2).broadcast_to([P, C, P]),
                                    v_unscale[:, 0:1], None, ALU.mult).then_inc(biases_ready, 1)
            split(2)
            split(3)
            dve.wait_ge(bv_projected, 1)
            dve.wait_ge(bf_loaded, 16)
            nc.vector.tensor_tensor(b_out[:], ps_ct[:, 0:H], bf_rows[:], ALU.add).then_inc(b_out_ready, 1)
            for g in FIRST[1:]:
                step(g, 0)
            with dve.Fori(0, REPS) as i:
                step(1, i)
                step(2, i)
            for g in LAST:
                step(g, 0)

        @block.tensor
        def _(pe):
            last_use = {}

            def wait_for_bank(kind, j, group, i):
                bank = BANK[kind, j]
                if bank in last_use:
                    was, item, of = last_use[bank]
                    if was == "qk":
                        pe.wait_ge(qk_stored, nth(QK, of, item, i))
                    if was == "v":
                        pe.wait_ge(v_split, nth(B, of, item, i))
                    if was == "ht":
                        pe.wait_ge(ht_split, nth(B, of, item, i))
                    if was == "f":
                        pe.wait_ge(y_ready, nth(B, of, item, i))
                last_use[bank] = kind, j, group
                return ps_proj[bank]

            def three_passes(out, a_hi, a_lo, b_hi, b_lo, first, last):
                nc.tensor.matmul(out, a_hi, b_hi, start=first, stop=False)
                nc.tensor.matmul(out, a_hi, b_lo, start=False, stop=False)
                return nc.tensor.matmul(out, a_lo, b_hi, start=False, stop=last)

            def transpose_normed(group, b, i):
                pe.wait_ge(h_ready, nth(B, group, b, i))
                ps = wait_for_bank("ht", b, group, i)
                for c in range(C):
                    last = nc.tensor.transpose(ps[:, c * N:(c + 1) * N], h_sb[:, b, c * P:(c + 1) * P], ident[:])
                last.then_inc(h_transposed, 1)

            def project_qk(group, j, i):
                w, m = divmod(j, C)
                if j == 0:
                    pe.wait_ge(ht_split, nth(B, group, B - 1, i))
                ps = wait_for_bank("qk", j, group, i)
                hi, lo = ht_hi[group % 2], ht_lo[group % 2]
                at = slice(m * P, (m + 1) * P)
                for c in range(C):
                    last = three_passes(ps[:], w_hi[w][:, c, at], w_lo[w][:, c, at], hi[:, c, :], lo[:, c, :],
                                        c == 0, c == C - 1)
                last.then_inc(qk_projected, 1)

            def project_v(group, b, i):
                ps = wait_for_bank("v", b, group, i)
                hi, lo = ht_hi[group % 2], ht_lo[group % 2]
                at = slice(b * N, (b + 1) * N)
                for c in range(C):
                    last = three_passes(ps[:, 0:H], hi[:, c, at], lo[:, c, at], w_hi[2][:, c, :], w_lo[2][:, c, :],
                                        c == 0, c == C - 1)
                last.then_inc(v_projected, 1)

            def scores(g, t, i):
                b, half = divmod(t, HALVES)
                if t == 0:
                    pe.wait_ge(qk_stored, nth(QK, g, QK - 1, i))
                if g >= 1 or t >= 2:
                    pe.wait_ge(scores_masked, nth(T, g, t - 2, i))
                rows, at = slice(half * D, (half + 1) * D), slice(b * N, (b + 1) * N)
                for k in range(K):
                    last = nc.tensor.matmul(ps_scores[t % 2][:, k * N:(k + 1) * N], qkt[g % 2][rows, k, at],
                                            qkt[g % 2][rows, C + k, at], start=True, stop=True)
                last.then_inc(scores_ready, 1)

            def transpose_probs(g, t, i):
                pe.wait_ge(probs_ready, nth(T, g, t, i))
                if g >= 1 or t >= 2:
                    pe.wait_ge(pt_split, nth(T, g, t - 2, i))
                for k in range(K):
                    last = nc.tensor.transpose(ps_pt[t % 2][:, k * N:(k + 1) * N], probs[t % 2][:, k, :], ident[:])
                last.then_inc(probs_transposed, 1)

            def weigh_values(g, t, i):
                b, half = divmod(t, HALVES)
                pe.wait_ge(pt_split, nth(T, g, t, i))
                if t == 0:
                    pe.wait_ge(v_split, nth(B, g, B - 1, i))
                if half == 0 and (g >= 1 or b >= 1):
                    pe.wait_ge(ctx_normalized, nth(B, g, b - 1, i))
                for k in range(K):
                    head = HALVES * k + half
                    at, nodes = slice(head * D, (head + 1) * D), slice(k * N, (k + 1) * N)
                    last = three_passes(ps_ctx[:, at], pt_hi[t % 2][:, nodes], pt_lo[t % 2][:, nodes],
                                        v_hi[g % 2][:, b, at], v_lo[g % 2][:, b, at], True, True)
                last.then_inc(values_weighted, 1)

            def transpose_ctx(g, b, i):
                pe.wait_ge(ctx_normalized, nth(B, g, b, i))
                if g == 0 and b == 0:
                    pe.wait_ge(b_out_ready, 1)
                else:
                    pe.wait_ge(ct_split, nth(B, g, b - 1, i))
                for c in range(C):
                    last = nc.tensor.transpose(ps_ct[:, c * P:(c + 1) * P], ctx_sb[b % 2][:, c * P:(c + 1) * P],
                                               ident[:])
                last.then_inc(ctx_transposed, 1)

            def project_out(g, b, i):
                pe.wait_ge(ct_split, nth(B, g, b, i))
                if g == 0 and b == 0:
                    pe.wait_ge(w_split, 4)
                ps = wait_for_bank("f", b, g, i)
                for c in range(C):
                    at = slice(c * P, (c + 1) * P)
                    last = three_passes(ps[:, 0:H], ct_hi[b % 2][:, at], ct_lo[b % 2][:, at],
                                        w_hi[3][:, c, :], w_lo[3][:, c, :], c == 0, c == C - 1)
                last.then_inc(y_projected, 1)

            def fill(g, uses, i):
                for kind, j in uses:
                    if kind == "qk" and projects(g):
                        project_qk(g + 1, j, i)
                    if kind == "v" and projects(g):
                        project_v(g + 1, j, i)
                    if kind == "ht" and norms(g):
                        transpose_normed(g + 2, j, i)

            def step(g, i):
                for n in range(SLOTS):
                    if attends(g) and n < T - 1:
                        scores(g, n + 1, i)
                    if projects(g) and n == SLOTS - 1:
                        scores(g + 1, 0, i)
                    if attends(g):
                        if 1 <= n <= T:
                            transpose_probs(g, n - 1, i)
                        if n % 2 and n >= 3:
                            transpose_ctx(g, (n - 3) // 2, i)
                    fill(g, FILL[n], i)
                    if attends(g):
                        if 1 <= n <= T:
                            weigh_values(g, n - 1, i)
                        if n % 2 and n >= 3:
                            project_out(g, (n - 3) // 2, i)
                    fill(g, FILL_LATE.get(n, []), i)

            pe.wait_ge(consts_set, 4)
            step(FIRST[0], 0)
            pe.wait_ge(biases_ready, 2)
            pe.wait_ge(w_scaled, 2)
            for c in range(C):
                last = nc.tensor.matmul(ps_ct[:, 0:H], bv_cols[:, c, :], w_raw[3][:, c, :],
                                        start=c == 0, stop=c == C - 1)
            last.then_inc(bv_projected, 1)
            pe.wait_ge(w_split, 3)
            for g in FIRST[1:]:
                step(g, 0)
            with pe.Fori(0, REPS) as i:
                step(1, i)
                step(2, i)
            for bank, (kind, j, group) in last_use.items():
                last_use[bank] = kind, j, group + 2 * (REPS - 1)
            for g in LAST:
                step(g, 0)


_INS = ["x", "adj", "L0_gnn_Wq", "L0_gnn_bq", "L0_gnn_Wk", "L0_gnn_bk", "L0_gnn_Wv", "L0_gnn_bv", "L0_gnn_Wf",
        "L0_gnn_bf"]


def kernel(**inputs):
    import numpy as _np
    import concourse.bacc as _bacc
    from concourse import mybir as _mybir
    from concourse.bass_utils import run_bass_kernel_spmd as _run

    nc = _bacc.Bacc("TRN2", target_bir_lowering=False, num_devices=1)
    arrays, args = {}, []
    for name in _INS:
        a = _np.ascontiguousarray(inputs[name])
        arrays[f"in_{name}"] = a
        args.append(nc.dram_tensor(f"in_{name}", a.shape, _mybir.dt.from_np(a.dtype), kind="ExternalInput").ap())
    y = nc.dram_tensor("y", (GRAPHS, N, H), _mybir.dt.float32, kind="ExternalOutput").ap()
    build(nc, *args, y)
    r = _run(nc, [arrays], core_ids=[0])
    return r.results[0]["y"]
```

```python
from contextlib import ExitStack

import concourse.bass as bass
from concourse import mybir

ALU = mybir.AluOpType
ACT = mybir.ActivationFunctionType
AX = mybir.AxisListType
F32 = mybir.dt.float32
F32R = mybir.dt.float32r
F16 = mybir.dt.float16
I32 = mybir.dt.int32
U8 = mybir.dt.uint8

P = 128
GRAPHS, N, H = 64, 128, 384
HEADS, D = 6, 64
C = H // P
B = 4
GROUPS = GRAPHS // B
HALVES = 2
K = HEADS // HALVES
T = B * HALVES
QK = 2 * C
EPS = 1e-5
NEG = -9000000000000000.0
SCALE = float(D) ** -0.5
TINY = 2.0 ** -100
EXPONENT_BITS = 0x7F800000

FIRST = (-2, -1, 0)
REPS = (GROUPS - 4) // 2
LAST = (GROUPS - 3, GROUPS - 2, GROUPS - 1)

STAGES = {
    "scores": (T, 0), "mask_and_max": (T, 0), "exponentials": (T, 0), "transpose_probs": (T, 0),
    "probs_hi": (T, 0), "probs_lo": (T, 0), "weigh_values": (T, 0), "normalize_ctx": (B, 0),
    "transpose_ctx": (B, 0), "ctx_hi": (B, 0), "ctx_lo": (B, 0), "project_out": (B, 0), "finish": (B, 0),
    "project_qk": (QK, 1), "store_qk": (QK, 1), "project_v": (B, 1), "values_hi": (B, 1), "values_lo": (B, 1),
    "statistics": (B, 2), "normalize": (B, 2), "transpose_normed": (B, 2), "normed_hi": (B, 2), "normed_lo": (B, 2),
}

TENSOR_ORDER = [
    ("project_qk", 0), ("transpose_probs", 3), ("scores", 6), ("transpose_ctx", 0), ("project_v", 0),
    ("project_qk", 1), ("project_qk", 2), ("project_qk", 3), ("weigh_values", 2), ("weigh_values", 3),
    ("transpose_probs", 4), ("project_v", 1), ("project_v", 2), ("scores", 7), ("transpose_probs", 5),
    ("project_qk", 4), ("project_qk", 5), ("transpose_ctx", 1), ("project_out", 0), ("scores", 8),
    ("weigh_values", 4), ("weigh_values", 5), ("transpose_probs", 6), ("transpose_normed", 0),
    ("transpose_probs", 7), ("scores", 9), ("project_v", 3), ("transpose_ctx", 2), ("scores", 10),
    ("transpose_normed", 1), ("weigh_values", 6), ("weigh_values", 7), ("transpose_probs", 8), ("scores", 11),
    ("project_out", 1), ("transpose_ctx", 3), ("transpose_probs", 9), ("project_out", 2), ("scores", 12),
    ("weigh_values", 8), ("transpose_normed", 2), ("transpose_normed", 3), ("transpose_probs", 10),
    ("weigh_values", 9), ("scores", 13), ("project_out", 3),
]
SCALAR_ORDER = [
    ("exponentials", 3), ("exponentials", 4), ("probs_hi", 3), ("store_qk", 0), ("values_hi", 0), ("store_qk", 1),
    ("store_qk", 2), ("exponentials", 5), ("store_qk", 3), ("ctx_hi", 0), ("probs_hi", 4), ("exponentials", 6),
    ("values_hi", 1), ("values_hi", 2), ("store_qk", 4), ("probs_hi", 5), ("ctx_hi", 1), ("store_qk", 5),
    ("exponentials", 7), ("probs_hi", 6), ("probs_hi", 7), ("normed_hi", 0), ("exponentials", 8), ("values_hi", 3),
    ("exponentials", 9), ("ctx_hi", 2), ("normed_hi", 1), ("probs_hi", 8), ("ctx_hi", 3), ("probs_hi", 9),
    ("exponentials", 10), ("normed_hi", 2), ("normed_hi", 3), ("probs_hi", 10),
]
VECTOR_ORDER = [
    ("statistics", 0), ("statistics", 1), ("values_lo", 0), ("probs_lo", 3), ("mask_and_max", 6),
    ("normalize_ctx", 1), ("statistics", 2), ("statistics", 3), ("ctx_lo", 0), ("mask_and_moments", 0),
    ("values_lo", 1), ("values_lo", 2), ("probs_lo", 4), ("mask_and_max", 7), ("normalize", 0), ("normalize", 1),
    ("probs_lo", 5), ("ctx_lo", 1), ("normalize", 2), ("normalize", 3), ("finish", 0), ("mask_and_max", 8),
    ("normalize_ctx", 2), ("probs_lo", 6), ("mask_and_max", 9), ("normed_lo", 0), ("probs_lo", 7), ("values_lo", 3),
    ("mask_and_max", 10), ("ctx_lo", 2), ("normed_lo", 1), ("normalize_ctx", 3), ("probs_lo", 8),
    ("mask_and_max", 11), ("finish", 1), ("ctx_lo", 3), ("probs_lo", 9), ("finish", 2), ("normed_lo", 2),
    ("normed_lo", 3), ("mask_and_max", 12), ("normalize_ctx", 4), ("probs_lo", 10), ("mask_and_max", 13),
    ("finish", 3),
]

AT_MOMENTS = VECTOR_ORDER.index(("mask_and_moments", 0))
VECTOR_BEFORE_MOMENTS, VECTOR_AFTER_MOMENTS = VECTOR_ORDER[:AT_MOMENTS], VECTOR_ORDER[AT_MOMENTS + 1:]

BANK_STAGES = ("project_qk", "project_v", "project_out", "transpose_normed")
BANK = {use: n % 2 for n, use in enumerate((stage, item % STAGES[stage][0]) for stage, item in TENSOR_ORDER
                                           if stage in BANK_STAGES)}


def items_of_step(order, g):
    for stage, item in order:
        count, ahead = STAGES[stage]
        group = g + ahead + item // count
        if 0 <= group < GROUPS:
            yield stage, group, item % count


def nth(per_group, group, item, i):
    return per_group * group + item + 1 + 2 * per_group * i


def loads(group, i):
    return 16 * (group // 2 + 1) + 16 * i


def projects(g):
    return 0 <= g + 1 < GROUPS


def norms(g):
    return 0 <= g + 2 < GROUPS


def build(nc, x, adj, wq, bq, wk, bk, wv, bv, wf, bf, out):
    x_v = x.rearrange("(g b) p h -> g p b h", b=B)
    adj_v = adj.rearrange("(g b) p k -> g p b k", b=B)
    out_v = out.rearrange("(g b) p h -> g p b h", b=B)

    ctx = ExitStack()
    with ctx:
        def sb(name, shape, dt=F32):
            return ctx.enter_context(nc.sbuf_tensor(name, shape, dt))

        def pb(name):
            return ctx.enter_context(nc.psum_tensor(name, [P, 512], F32))

        def sem(name):
            return ctx.enter_context(nc.semaphore(name))

        w_raw = [sb(f"w_raw{n}", [P, C, H]) for n in range(4)]
        w_hi = [sb(f"w_hi{n}", [P, C, H], F32R) for n in range(4)]
        w_lo = [sb(f"w_lo{n}", [P, C, H], F32R) for n in range(4)]
        bias_raw = sb("bias_raw", [P, 3, C])
        bias_qk = sb("bias_qk", [P, QK])
        bv_cols = sb("bv_cols", [P, C, P])
        bf_rows = sb("bf_rows", [P, H])
        b_out = sb("b_out", [P, H])
        wv_most = sb("wv_most", [P, 1])
        wv_most_all = sb("wv_most_all", [P, 1])
        wv_bound = sb("wv_bound", [P, 1])
        v_scale = sb("v_scale", [P, 1])
        v_unscale = sb("v_unscale", [P, 1])
        ident = sb("ident", [P, P])
        minus_half = sb("minus_half", [P, B])
        eps = sb("eps", [P, B])
        x_sb = [sb(f"x_sb{n}", [P, B, H]) for n in range(2)]
        x_bf = [sb(f"x_bf{n}", [P, B, H]) for n in range(2)]
        adj_sb = [sb(f"adj_sb{n}", [P, B, N], U8) for n in range(2)]
        mask = [sb(f"mask{n}", [P, B, N]) for n in range(2)]
        ht_hi = [sb(f"ht_hi{n}", [P, C, B * N], F32R) for n in range(2)]
        ht_lo = [sb(f"ht_lo{n}", [P, C, B * N], F32R) for n in range(2)]
        qkt = [sb(f"qkt{n}", [P, QK, B * N]) for n in range(2)]
        v_hi = [sb(f"v_hi{n}", [P, B, H], F16) for n in range(2)]
        v_lo = [sb(f"v_lo{n}", [P, B, H], F16) for n in range(2)]
        stats = sb("stats", [P, B, 6])
        moments = sb("moments", [P, B, 2])
        var_eps = sb("var_eps", [P, B])
        rstd = sb("rstd", [P, B])
        h_sb = sb("h_sb", [P, B, H])
        masked = [sb(f"masked{n}", [P, K, N]) for n in range(2)]
        neg_max = [sb(f"neg_max{n}", [P, K]) for n in range(2)]
        probs = [sb(f"probs{n}", [P, K, N]) for n in range(2)]
        pt_hi = [sb(f"pt_hi{n}", [P, K * N], F16) for n in range(2)]
        pt_lo = [sb(f"pt_lo{n}", [P, K * N], F16) for n in range(2)]
        sums = [sb(f"sums{n}", [P, HEADS]) for n in range(2)]
        inv_sums = [sb(f"inv_sums{n}", [P, HEADS]) for n in range(2)]
        ctx_sb = [sb(f"ctx_sb{n}", [P, H]) for n in range(2)]
        ct_hi = [sb(f"ct_hi{n}", [P, H], F32R) for n in range(2)]
        ct_lo = [sb(f"ct_lo{n}", [P, H], F32R) for n in range(2)]
        y_sb = [sb(f"y_sb{n}", [P, H]) for n in range(2)]

        ps_proj = [pb(f"ps_proj{n}") for n in range(2)]
        ps_scores = [pb(f"ps_scores{n}") for n in range(2)]
        ps_pt = [pb(f"ps_pt{n}") for n in range(2)]
        ps_ctx = pb("ps_ctx")
        ps_ct = pb("ps_ct")

        x_loaded = [sem(f"x_loaded{n}") for n in range(2)]
        adj_loaded = [sem(f"adj_loaded{n}") for n in range(2)]
        w_loaded = [sem(f"w_loaded{n}") for n in range(4)]
        bias_loaded = sem("bias_loaded")
        bf_loaded = sem("bf_loaded")
        y_stored = [sem(f"y_stored{n}") for n in range(2)]
        consts_set = sem("consts_set")
        wv_reduced = sem("wv_reduced")
        wv_reduced_all = sem("wv_reduced_all")
        v_scale_step = sem("v_scale_step")
        w_scaled = sem("w_scaled")
        w_hi_ready = sem("w_hi_ready")
        w_split = sem("w_split")
        biases_ready = sem("biases_ready")
        bv_projected = sem("bv_projected")
        b_out_ready = sem("b_out_ready")
        stats_ready = sem("stats_ready")
        moments_ready = sem("moments_ready")
        var_eps_ready = sem("var_eps_ready")
        rstd_ready = sem("rstd_ready")
        h_ready = sem("h_ready")
        x_bf_ready = sem("x_bf_ready")
        mask_ready = sem("mask_ready")
        h_transposed = sem("h_transposed")
        ht_hi_ready = sem("ht_hi_ready")
        ht_split = sem("ht_split")
        qk_projected = sem("qk_projected")
        qk_stored = sem("qk_stored")
        v_projected = sem("v_projected")
        v_hi_ready = sem("v_hi_ready")
        v_split = sem("v_split")
        scores_ready = sem("scores_ready")
        scores_masked = sem("scores_masked")
        max_ready = sem("max_ready")
        probs_ready = sem("probs_ready")
        probs_transposed = sem("probs_transposed")
        pt_hi_ready = sem("pt_hi_ready")
        pt_split = sem("pt_split")
        values_weighted = sem("values_weighted")
        sums_inverted = sem("sums_inverted")
        ctx_normalized = sem("ctx_normalized")
        ctx_transposed = sem("ctx_transposed")
        ct_hi_ready = sem("ct_hi_ready")
        ct_split = sem("ct_split")
        y_projected = sem("y_projected")
        y_ready = sem("y_ready")

        block = ctx.enter_context(nc.Block())

        @block.sync
        def _(sp):
            def step(g, i):
                if g >= 0:
                    for b in range(B):
                        sp.wait_ge(y_ready, nth(B, g, b, i))
                        sp.dma_start(out_v[g + 2 * i, :, b, :], y_sb[b % 2][:]).then_inc(y_stored[b % 2], 16)

            for n, w in enumerate((wq, wk, wv, wf)):
                sp.dma_start(w_raw[n][:], w.rearrange("(c p) n -> p c n", p=P)).then_inc(w_loaded[n], 16)
            for g in FIRST:
                step(g, 0)
            with sp.Fori(0, REPS) as i:
                step(1, i)
                step(2, i)
            for g in LAST:
                step(g, 0)
            for n in range(2):
                sp.wait_ge(y_stored[n], 16 * GRAPHS // 2)

        @block.gpsimd
        def _(pool):
            def inverse_deviation(group, i):
                pool.wait_ge(moments_ready, nth(1, group, 0, i))
                nc.gpsimd.tensor_tensor(var_eps[:], moments[:, :, 1], eps[:], ALU.add).then_inc(var_eps_ready, 1)
                pool.wait_ge(var_eps_ready, nth(1, group, 0, i))
                if group >= 1:
                    pool.wait_ge(h_ready, nth(B, group - 1, B - 1, i))
                nc.gpsimd.tensor_tensor(rstd[:], var_eps[:], minus_half[:], ALU.pow).then_inc(rstd_ready, 1)

            def residual(group, i):
                par = group % 2
                pool.wait_ge(x_loaded[par], loads(group, i))
                if group >= 2:
                    pool.wait_ge(y_ready, nth(B, group - 2, B - 1, i))
                nc.gpsimd.tensor_tensor(x_bf[par][:], x_sb[par][:],
                                        b_out[:].unsqueeze(1).broadcast_to([P, B, H]), ALU.add)\
                    .then_inc(x_bf_ready, 1)

            def step(g, i):
                if norms(g):
                    inverse_deviation(g + 2, i)
                if projects(g):
                    residual(g + 1, i)

            nc.gpsimd.memset(minus_half[:], -0.5).then_inc(consts_set, 1)
            nc.gpsimd.memset(eps[:], EPS).then_inc(consts_set, 1)
            nc.gpsimd.memset(ident[:], 0.0).then_inc(consts_set, 1)
            pool.wait_ge(consts_set, 3)
            nc.gpsimd.affine_select(out=ident[:], in_=ident[:], compare_op=ALU.not_equal, fill=1.0, base=0,
                                    pattern=[[-1, P]], channel_multiplier=1).then_inc(consts_set, 1)
            step(FIRST[0], 0)
            pool.wait_ge(wv_reduced, 1)
            nc.gpsimd.partition_all_reduce(wv_most_all[:], wv_most[:], P, bass.bass_isa.ReduceOp.max)\
                .then_inc(wv_reduced_all, 1)
            pool.wait_ge(b_out_ready, 1)
            for g in FIRST[1:]:
                step(g, 0)
            with pool.Fori(0, REPS) as i:
                step(1, i)
                step(2, i)
            for g in LAST:
                step(g, 0)

        @block.scalar
        def _(act):
            def load(group, i):
                par = group % 2
                if group >= 2:
                    act.wait_ge(h_ready, nth(B, group - 2, B - 1, i))
                    act.wait_ge(x_bf_ready, nth(1, group - 2, 0, i))
                    act.wait_ge(mask_ready, nth(1, group - 2, 0, i))
                at = group + 2 * i
                act.dma_start(x_sb[par][:], x_v[at, :, :, :]).then_inc(x_loaded[par], 16)
                act.dma_start(adj_sb[par][:], adj_v[at, :, :, :]).then_inc(adj_loaded[par], 16)

            def exponentials(g, t, i):
                b, half = divmod(t, HALVES)
                act.wait_ge(max_ready, nth(T, g, t, i))
                if g >= 1 or t >= 2:
                    act.wait_ge(probs_transposed, nth(T, g, t - 2, i))
                if g >= 1 or b >= 2:
                    act.wait_ge(sums_inverted, nth(B, g, b - 2, i))
                for k in range(K):
                    head = HALVES * k + half
                    last = nc.scalar.activation(probs[t % 2][:, k, :], masked[t % 2][:, k, :], ACT.Exp,
                                                bias=neg_max[t % 2][:, k:k + 1],
                                                accum_out=sums[b % 2][:, head:head + 1])
                last.then_inc(probs_ready, 1)

            def probs_hi(g, t, i):
                act.wait_ge(probs_transposed, nth(T, g, t, i))
                if g >= 1 or t >= 2:
                    act.wait_ge(values_weighted, nth(T, g, t - 2, i))
                nc.scalar.activation(pt_hi[t % 2][:], ps_pt[t % 2][:, 0:K * N], ACT.Copy).then_inc(pt_hi_ready, 1)

            def ctx_hi(g, b, i):
                act.wait_ge(ctx_transposed, nth(B, g, b, i))
                if g >= 1 or b >= 2:
                    act.wait_ge(y_projected, nth(B, g, b - 2, i))
                nc.scalar.activation(ct_hi[b % 2][:], ps_ct[:, 0:H], ACT.Copy).then_inc(ct_hi_ready, 1)

            def store_qk(group, j, i):
                act.wait_ge(qk_projected, nth(QK, group, j, i))
                if group == 0 and j == 0:
                    act.wait_ge(biases_ready, 1)
                if group >= 2 and j == 0:
                    act.wait_ge(scores_ready, nth(T, group - 2, T - 1, i))
                nc.scalar.activation(qkt[group % 2][:, j, :], ps_proj[BANK["project_qk", j]][:], ACT.Identity,
                                     bias=bias_qk[:, j:j + 1], scale=SCALE if j < C else 1.0)\
                    .then_inc(qk_stored, 1)

            def values_hi(group, b, i):
                act.wait_ge(v_projected, nth(B, group, b, i))
                if group >= 2 and b == 0:
                    act.wait_ge(values_weighted, nth(T, group - 2, T - 1, i))
                nc.scalar.activation(v_hi[group % 2][:, b, :], ps_proj[BANK["project_v", b]][:, 0:H], ACT.Copy)\
                    .then_inc(v_hi_ready, 1)

            def normed_hi(group, b, i):
                act.wait_ge(h_transposed, nth(B, group, b, i))
                if group >= 2 and b == 0:
                    act.wait_ge(qk_projected, nth(QK, group - 2, QK - 1, i))
                    act.wait_ge(v_projected, nth(B, group - 2, B - 1, i))
                nc.scalar.activation(ht_hi[group % 2][:, :, b * N:(b + 1) * N],
                                     ps_proj[BANK["transpose_normed", b]][:, 0:H].rearrange("p (c n) -> p c n", c=C),
                                     ACT.Relu).then_inc(ht_hi_ready, 1)

            stages = {"exponentials": exponentials, "probs_hi": probs_hi, "ctx_hi": ctx_hi, "store_qk": store_qk,
                      "values_hi": values_hi, "normed_hi": normed_hi}

            def step(g, i):
                for stage, group, item in items_of_step(SCALAR_ORDER, g):
                    stages[stage](group, item, i)
                if g + 3 < GROUPS:
                    load(g + 3, i)

            load(0, 0)
            act.dma_start(bias_raw[:, 0, :], bq.rearrange("(c p) -> p c", p=P), allow_slow_non_contiguous=True)\
                .then_inc(bias_loaded, 16)
            act.dma_start(bias_raw[:, 1, :], bk.rearrange("(c p) -> p c", p=P), allow_slow_non_contiguous=True)\
                .then_inc(bias_loaded, 16)
            act.dma_start(bias_raw[:, 2, :], bv.rearrange("(c p) -> p c", p=P), allow_slow_non_contiguous=True)\
                .then_inc(bias_loaded, 16)
            act.dma_start(bf_rows[:], bf.partition_broadcast(P)).then_inc(bf_loaded, 16)
            step(FIRST[0], 0)
            for n in range(4):
                act.wait_ge(w_loaded[n], 16)
                if n >= 2:
                    act.wait_ge(w_scaled, n - 1)
                nc.scalar.activation(w_hi[n][:], w_raw[n][:], ACT.Copy).then_inc(w_hi_ready, 1)
            for g in FIRST[1:]:
                step(g, 0)
            with act.Fori(0, REPS) as i:
                step(1, i)
                step(2, i)
            for g in LAST:
                step(g, 0)

        @block.vector
        def _(dve):
            def statistics(group, b, i):
                if b == 0:
                    dve.wait_ge(x_loaded[group % 2], loads(group, i))
                    if group >= 1:
                        dve.wait_ge(moments_ready, nth(1, group - 1, 0, i))
                nc.vector.bn_stats(stats[:, b, :], x_sb[group % 2][:, b, :]).then_inc(stats_ready, 1)

            def additive_mask(group, i):
                dve.wait_ge(adj_loaded[group % 2], loads(group, i))
                if group >= 2:
                    dve.wait_ge(scores_masked, nth(T, group - 2, T - 1, i))
                nc.vector.tensor_scalar(mask[group % 2][:], adj_sb[group % 2][:], -NEG, NEG, ALU.mult, ALU.add)\
                    .then_inc(mask_ready, 1)

            def wait_to_aggregate(group, i):
                dve.wait_ge(stats_ready, nth(B, group, B - 1, i))
                if group >= 1:
                    dve.wait_ge(h_ready, nth(B, group - 1, B - 1, i))
                    dve.wait_ge(var_eps_ready, nth(1, group - 1, 0, i))

            def aggregate(group):
                for b in range(B):
                    last = nc.vector.bn_aggr(moments[:, b, :], stats[:, b, :])
                last.then_inc(moments_ready, 1)

            def normalize(group, b, i):
                dve.wait_ge(rstd_ready, nth(1, group, 0, i))
                if group >= 1:
                    dve.wait_ge(h_transposed, nth(B, group - 1, b, i))
                nc.vector.tensor_scalar(h_sb[:, b, :], x_sb[group % 2][:, b, :], moments[:, b, 0:1],
                                        rstd[:, b:b + 1], ALU.subtract, ALU.mult).then_inc(h_ready, 1)

            def mask_and_max(g, t, i):
                dve.wait_ge(scores_ready, nth(T, g, t, i))
                dve.wait_ge(mask_ready, nth(1, g, 0, i))
                if g >= 1 or t >= 2:
                    dve.wait_ge(probs_ready, nth(T, g, t - 2, i))
                nc.vector.tensor_tensor(masked[t % 2][:],
                                        ps_scores[t % 2][:, 0:K * N].rearrange("p (k n) -> p k n", k=K),
                                        mask[g % 2][:, t // HALVES, :].unsqueeze(1).broadcast_to([P, K, N]),
                                        ALU.add).then_inc(scores_masked, 1)
                dve.wait_ge(scores_masked, nth(T, g, t, i))
                nc.vector.tensor_reduce(neg_max[t % 2][:], masked[t % 2][:], AX.X, ALU.max, negate=True)\
                    .then_inc(max_ready, 1)

            def probs_lo(g, t, i):
                dve.wait_ge(pt_hi_ready, nth(T, g, t, i))
                nc.vector.tensor_tensor(pt_lo[t % 2][:], ps_pt[t % 2][:, 0:K * N], pt_hi[t % 2][:], ALU.subtract)\
                    .then_inc(pt_split, 1)

            def normalize_ctx(g, b, i):
                dve.wait_ge(probs_ready, nth(T, g, HALVES * b + 1, i))
                if g >= 1 or b >= 2:
                    dve.wait_ge(ctx_normalized, nth(B, g, b - 2, i))
                nc.vector.reciprocal(inv_sums[b % 2][:], sums[b % 2][:]).then_inc(sums_inverted, 1)
                dve.wait_ge(sums_inverted, nth(B, g, b, i))
                dve.wait_ge(values_weighted, nth(T, g, HALVES * b + 1, i))
                if g >= 1 or b >= 2:
                    dve.wait_ge(ctx_transposed, nth(B, g, b - 2, i))
                nc.vector.tensor_tensor(ctx_sb[b % 2][:].rearrange("p (h d) -> p h d", h=HEADS),
                                        ps_ctx[:, 0:H].rearrange("p (h d) -> p h d", h=HEADS),
                                        inv_sums[b % 2][:].unsqueeze(2).broadcast_to([P, HEADS, D]),
                                        ALU.mult).then_inc(ctx_normalized, 1)

            def ctx_lo(g, b, i):
                dve.wait_ge(ct_hi_ready, nth(B, g, b, i))
                nc.vector.tensor_tensor(ct_lo[b % 2][:], ps_ct[:, 0:H], ct_hi[b % 2][:].bitcast(F32), ALU.subtract)\
                    .then_inc(ct_split, 1)

            def finish(g, b, i):
                dve.wait_ge(y_projected, nth(B, g, b, i))
                dve.wait_ge(x_bf_ready, nth(1, g, 0, i))
                if g >= 1 or b >= 2:
                    dve.wait_ge(y_stored[b % 2], 16 * (2 * g + b // 2) + 64 * i)
                nc.vector.tensor_tensor(y_sb[b % 2][:], ps_proj[BANK["project_out", b]][:, 0:H], x_bf[g % 2][:, b, :],
                                        ALU.add).then_inc(y_ready, 1)

            def values_lo(group, b, i):
                dve.wait_ge(v_hi_ready, nth(B, group, b, i))
                nc.vector.tensor_tensor(v_lo[group % 2][:, b, :], ps_proj[BANK["project_v", b]][:, 0:H],
                                        v_hi[group % 2][:, b, :], ALU.subtract).then_inc(v_split, 1)

            def normed_lo(group, b, i):
                dve.wait_ge(ht_hi_ready, nth(B, group, b, i))
                at = slice(b * N, (b + 1) * N)
                nc.vector.scalar_tensor_tensor(out=ht_lo[group % 2][:, :, at],
                                               in0=ps_proj[BANK["transpose_normed", b]][:, 0:H].rearrange("p (c n) -> p c n", c=C),
                                               scalar=0.0, in1=ht_hi[group % 2][:, :, at].bitcast(F32),
                                               op0=ALU.max, op1=ALU.subtract).then_inc(ht_split, 1)

            def mask_and_moments(g, i):
                if norms(g):
                    wait_to_aggregate(g + 2, i)
                if projects(g):
                    additive_mask(g + 1, i)
                if norms(g):
                    aggregate(g + 2)

            stages = {"mask_and_max": mask_and_max, "probs_lo": probs_lo, "normalize_ctx": normalize_ctx,
                      "ctx_lo": ctx_lo, "finish": finish, "values_lo": values_lo, "statistics": statistics,
                      "normalize": normalize, "normed_lo": normed_lo}

            def step(g, i):
                for stage, group, item in items_of_step(VECTOR_BEFORE_MOMENTS, g):
                    stages[stage](group, item, i)
                mask_and_moments(g, i)
                for stage, group, item in items_of_step(VECTOR_AFTER_MOMENTS, g):
                    stages[stage](group, item, i)

            def split(n):
                dve.wait_ge(w_hi_ready, n + 1)
                nc.vector.tensor_tensor(w_lo[n][:], w_raw[n][:], w_hi[n][:].bitcast(F32), ALU.subtract)\
                    .then_inc(w_split, 1)

            step(FIRST[0], 0)
            dve.wait_ge(w_loaded[2], 16)
            nc.vector.tensor_reduce(wv_most[:], w_raw[2][:], AX.XY, ALU.max, apply_absolute_value=True)\
                .then_inc(wv_reduced, 1)
            split(0)
            split(1)
            dve.wait_ge(wv_reduced_all, 1)
            nc.vector.tensor_scalar(wv_bound[:], wv_most_all[:], TINY, None, ALU.max).then_inc(v_scale_step, 1)
            dve.wait_ge(v_scale_step, 1)
            nc.vector.tensor_scalar(v_scale[:].bitcast(I32), wv_bound[:].bitcast(I32), EXPONENT_BITS, None,
                                    ALU.bitwise_and).then_inc(v_scale_step, 1)
            dve.wait_ge(v_scale_step, 2)
            nc.vector.reciprocal(v_unscale[:], v_scale[:]).then_inc(v_scale_step, 1)
            dve.wait_ge(v_scale_step, 3)
            nc.vector.tensor_scalar(w_raw[2][:], w_raw[2][:], v_unscale[:, 0:1], None, ALU.mult).then_inc(w_scaled, 1)
            dve.wait_ge(w_loaded[3], 16)
            nc.vector.tensor_scalar(w_raw[3][:], w_raw[3][:], v_scale[:, 0:1], None, ALU.mult).then_inc(w_scaled, 1)
            dve.wait_ge(bias_loaded, 48)
            nc.vector.tensor_scalar(bias_qk[:, 0:C], bias_raw[:, 0, :], SCALE, None, ALU.mult)
            nc.vector.tensor_copy(bias_qk[:, C:QK], bias_raw[:, 1, :]).then_inc(biases_ready, 1)
            nc.vector.tensor_scalar(bv_cols[:], bias_raw[:, 2, :].unsqueeze(2).broadcast_to([P, C, P]),
                                    v_unscale[:, 0:1], None, ALU.mult).then_inc(biases_ready, 1)
            split(2)
            split(3)
            dve.wait_ge(bv_projected, 1)
            dve.wait_ge(bf_loaded, 16)
            nc.vector.tensor_tensor(b_out[:], ps_ct[:, 0:H], bf_rows[:], ALU.add).then_inc(b_out_ready, 1)
            for g in FIRST[1:]:
                step(g, 0)
            with dve.Fori(0, REPS) as i:
                step(1, i)
                step(2, i)
            for g in LAST:
                step(g, 0)

        @block.tensor
        def _(pe):
            last_use = {}

            def wait_for_bank(kind, j, group, i):
                bank = BANK[kind, j]
                if bank in last_use:
                    was, item, of = last_use[bank]
                    if was == "project_qk":
                        pe.wait_ge(qk_stored, nth(QK, of, item, i))
                    if was == "project_v":
                        pe.wait_ge(v_split, nth(B, of, item, i))
                    if was == "transpose_normed":
                        pe.wait_ge(ht_split, nth(B, of, item, i))
                    if was == "project_out":
                        pe.wait_ge(y_ready, nth(B, of, item, i))
                last_use[bank] = kind, j, group
                return ps_proj[bank]

            def three_passes(out, a_hi, a_lo, b_hi, b_lo, first, last):
                nc.tensor.matmul(out, a_hi, b_hi, start=first, stop=False)
                nc.tensor.matmul(out, a_hi, b_lo, start=False, stop=False)
                return nc.tensor.matmul(out, a_lo, b_hi, start=False, stop=last)

            def transpose_normed(group, b, i):
                pe.wait_ge(h_ready, nth(B, group, b, i))
                ps = wait_for_bank("transpose_normed", b, group, i)
                for c in range(C):
                    last = nc.tensor.transpose(ps[:, c * N:(c + 1) * N], h_sb[:, b, c * P:(c + 1) * P], ident[:])
                last.then_inc(h_transposed, 1)

            def project_qk(group, j, i):
                w, m = divmod(j, C)
                if j == 0:
                    pe.wait_ge(ht_split, nth(B, group, B - 1, i))
                ps = wait_for_bank("project_qk", j, group, i)
                hi, lo = ht_hi[group % 2], ht_lo[group % 2]
                at = slice(m * P, (m + 1) * P)
                for c in range(C):
                    last = three_passes(ps[:], w_hi[w][:, c, at], w_lo[w][:, c, at], hi[:, c, :], lo[:, c, :],
                                        c == 0, c == C - 1)
                last.then_inc(qk_projected, 1)

            def project_v(group, b, i):
                ps = wait_for_bank("project_v", b, group, i)
                hi, lo = ht_hi[group % 2], ht_lo[group % 2]
                at = slice(b * N, (b + 1) * N)
                for c in range(C):
                    last = three_passes(ps[:, 0:H], hi[:, c, at], lo[:, c, at], w_hi[2][:, c, :], w_lo[2][:, c, :],
                                        c == 0, c == C - 1)
                last.then_inc(v_projected, 1)

            def scores(g, t, i):
                b, half = divmod(t, HALVES)
                if t == 0:
                    pe.wait_ge(qk_stored, nth(QK, g, QK - 1, i))
                if g >= 1 or t >= 2:
                    pe.wait_ge(scores_masked, nth(T, g, t - 2, i))
                rows, at = slice(half * D, (half + 1) * D), slice(b * N, (b + 1) * N)
                for k in range(K):
                    last = nc.tensor.matmul(ps_scores[t % 2][:, k * N:(k + 1) * N], qkt[g % 2][rows, k, at],
                                            qkt[g % 2][rows, C + k, at], start=True, stop=True)
                last.then_inc(scores_ready, 1)

            def transpose_probs(g, t, i):
                pe.wait_ge(probs_ready, nth(T, g, t, i))
                if g >= 1 or t >= 2:
                    pe.wait_ge(pt_split, nth(T, g, t - 2, i))
                for k in range(K):
                    last = nc.tensor.transpose(ps_pt[t % 2][:, k * N:(k + 1) * N], probs[t % 2][:, k, :], ident[:])
                last.then_inc(probs_transposed, 1)

            def weigh_values(g, t, i):
                b, half = divmod(t, HALVES)
                pe.wait_ge(pt_split, nth(T, g, t, i))
                if t == 0:
                    pe.wait_ge(v_split, nth(B, g, B - 1, i))
                if half == 0 and (g >= 1 or b >= 1):
                    pe.wait_ge(ctx_normalized, nth(B, g, b - 1, i))
                for k in range(K):
                    head = HALVES * k + half
                    at, nodes = slice(head * D, (head + 1) * D), slice(k * N, (k + 1) * N)
                    last = three_passes(ps_ctx[:, at], pt_hi[t % 2][:, nodes], pt_lo[t % 2][:, nodes],
                                        v_hi[g % 2][:, b, at], v_lo[g % 2][:, b, at], True, True)
                last.then_inc(values_weighted, 1)

            def transpose_ctx(g, b, i):
                pe.wait_ge(ctx_normalized, nth(B, g, b, i))
                if g == 0 and b == 0:
                    pe.wait_ge(b_out_ready, 1)
                else:
                    pe.wait_ge(ct_split, nth(B, g, b - 1, i))
                for c in range(C):
                    last = nc.tensor.transpose(ps_ct[:, c * P:(c + 1) * P], ctx_sb[b % 2][:, c * P:(c + 1) * P],
                                               ident[:])
                last.then_inc(ctx_transposed, 1)

            def project_out(g, b, i):
                pe.wait_ge(ct_split, nth(B, g, b, i))
                if g == 0 and b == 0:
                    pe.wait_ge(w_split, 4)
                ps = wait_for_bank("project_out", b, g, i)
                for c in range(C):
                    at = slice(c * P, (c + 1) * P)
                    last = three_passes(ps[:, 0:H], ct_hi[b % 2][:, at], ct_lo[b % 2][:, at],
                                        w_hi[3][:, c, :], w_lo[3][:, c, :], c == 0, c == C - 1)
                last.then_inc(y_projected, 1)

            stages = {"scores": scores, "transpose_probs": transpose_probs, "weigh_values": weigh_values,
                      "transpose_ctx": transpose_ctx, "project_out": project_out, "project_qk": project_qk,
                      "project_v": project_v, "transpose_normed": transpose_normed}

            def step(g, i):
                for stage, group, item in items_of_step(TENSOR_ORDER, g):
                    stages[stage](group, item, i)

            pe.wait_ge(consts_set, 4)
            step(FIRST[0], 0)
            pe.wait_ge(biases_ready, 2)
            pe.wait_ge(w_scaled, 2)
            for c in range(C):
                last = nc.tensor.matmul(ps_ct[:, 0:H], bv_cols[:, c, :], w_raw[3][:, c, :],
                                        start=c == 0, stop=c == C - 1)
            last.then_inc(bv_projected, 1)
            pe.wait_ge(w_split, 3)
            for g in FIRST[1:]:
                step(g, 0)
            with pe.Fori(0, REPS) as i:
                step(1, i)
                step(2, i)
            for bank, (kind, j, group) in last_use.items():
                last_use[bank] = kind, j, group + 2 * (REPS - 1)
            for g in LAST:
                step(g, 0)


_INS = ["x", "adj", "L0_gnn_Wq", "L0_gnn_bq", "L0_gnn_Wk", "L0_gnn_bk", "L0_gnn_Wv", "L0_gnn_bv", "L0_gnn_Wf",
        "L0_gnn_bf"]


def kernel(**inputs):
    import numpy as _np
    import concourse.bacc as _bacc
    from concourse import mybir as _mybir
    from concourse.bass_utils import run_bass_kernel_spmd as _run

    nc = _bacc.Bacc("TRN2", target_bir_lowering=False, num_devices=1)
    arrays, args = {}, []
    for name in _INS:
        a = _np.ascontiguousarray(inputs[name])
        arrays[f"in_{name}"] = a
        args.append(nc.dram_tensor(f"in_{name}", a.shape, _mybir.dt.from_np(a.dtype), kind="ExternalInput").ap())
    y = nc.dram_tensor("y", (GRAPHS, N, H), _mybir.dt.float32, kind="ExternalOutput").ap()
    build(nc, *args, y)
    r = _run(nc, [arrays], core_ids=[0])
    return r.results[0]["y"]
```

```python
from contextlib import ExitStack

import concourse.bass as bass
from concourse import mybir

ALU = mybir.AluOpType
ACT = mybir.ActivationFunctionType
AX = mybir.AxisListType
F32 = mybir.dt.float32
F16 = mybir.dt.float16
I32 = mybir.dt.int32
U8 = mybir.dt.uint8

P = 128
GRAPHS, N, H = 64, 128, 384
HEADS, D = 6, 64
C = H // P
B = 4
GROUPS = GRAPHS // B
HALVES = 2
K = HEADS // HALVES
T = B * HALVES
QK = 2 * C
EPS = 1e-5
NEG = -9000000000000000.0
SCALE = float(D) ** -0.5
TINY = 2.0 ** -100
PARTS = 2
UNITS = 4
PROJ_BANKS = 4
SCALE_STEPS = 3
WEIGHT_MOST = 64.0
EXPONENT_BITS = 0x7F800000

REPS = (GROUPS - 4) // 2
LAST = (GROUPS - 3, GROUPS - 2, GROUPS - 1)

STAGES = {
    "scores": (T, 0), "mask_and_max": (T, 0), "exponentials": (T, 0), "transpose_probs": (T, 0),
    "probs_hi": (T, 0), "probs_lo": (T, 0), "weigh_values": (T, 0), "normalize_ctx": (B, 0),
    "transpose_ctx": (B, 0), "ctx_hi": (B, 0), "ctx_lo": (B, 0), "project_out": (B, 0), "finish": (B, 0),
    "store": (B, 0),
    "project_qk": (QK, 1), "qk_hi": (QK, 1), "qk_lo": (QK, 1), "project_v": (B, 1),
    "values_hi": (B, 1), "values_lo": (B, 1),
    "residual": (B, 1), "statistics": (B, 2), "inverse_deviation": (1, 2), "normalize": (B, 2),
    "transpose_normed": (B, 2), "normed_hi": (B, 2), "normed_lo": (B, 2), "load": (B, 3),
}

TENSOR_ORDER = [
    ("project_qk", 0), ("scores", 6), ("project_qk", 1), ("weigh_values", 0), ("scores", 7), ("weigh_values", 1),
    ("project_qk", 2), ("project_qk", 3), ("weigh_values", 2), ("weigh_values", 3), ("project_qk", 4),
    ("weigh_values", 4), ("project_qk", 5), ("project_v", 0), ("weigh_values", 5), ("project_out", 0),
    ("scores", 8), ("weigh_values", 6), ("weigh_values", 7), ("project_v", 1), ("scores", 9), ("project_out", 1),
    ("scores", 10), ("project_v", 2), ("scores", 11), ("project_out", 2), ("scores", 12), ("project_v", 3),
    ("scores", 13), ("project_out", 3),
]
SCALAR_ORDER = [
    ("exponentials", 5), ("qk_hi", 0), ("probs_hi", 5), ("exponentials", 6), ("load", 0), ("qk_hi", 1),
    ("qk_hi", 2), ("ctx_hi", 0), ("probs_hi", 6), ("normed_hi", 0), ("exponentials", 7), ("qk_hi", 3),
    ("probs_hi", 7), ("ctx_hi", 1), ("normed_hi", 1), ("load", 1), ("qk_hi", 4), ("qk_hi", 5), ("normed_hi", 2),
    ("values_hi", 0), ("ctx_hi", 2), ("load", 2), ("load", 3), ("normed_hi", 3), ("ctx_hi", 3), ("values_hi", 1),
    ("exponentials", 8), ("probs_hi", 8), ("exponentials", 9), ("probs_hi", 9), ("values_hi", 2),
    ("exponentials", 10), ("exponentials", 11), ("probs_hi", 10), ("values_hi", 3), ("probs_hi", 11),
    ("exponentials", 12), ("probs_hi", 12),
]
VECTOR_ORDER = [
    ("statistics", 0), ("statistics", 1), ("statistics", 2), ("statistics", 3), ("mask_and_max", 6),
    ("mask_and_moments", 0), ("normalize_ctx", 0), ("qk_lo", 0), ("mask_and_max", 7), ("normalize", 0),
    ("normalize", 1), ("qk_lo", 1), ("ctx_lo", 0), ("qk_lo", 2), ("normed_lo", 0), ("normalize_ctx", 1),
    ("normalize", 2), ("qk_lo", 3), ("ctx_lo", 1), ("normed_lo", 1), ("qk_lo", 4), ("qk_lo", 5),
    ("normalize_ctx", 2), ("normed_lo", 2), ("normalize", 3), ("values_lo", 0), ("ctx_lo", 2), ("normalize_ctx", 3),
    ("mask_and_max", 8), ("normed_lo", 3), ("mask_and_max", 9), ("finish", 0), ("ctx_lo", 3), ("mask_and_max", 10),
    ("values_lo", 1), ("mask_and_max", 11), ("finish", 1), ("values_lo", 2), ("finish", 2), ("mask_and_max", 12),
    ("mask_and_max", 13), ("values_lo", 3), ("finish", 3),
]
SYNC_ORDER = [
    ("transpose_probs", 6), ("transpose_probs", 7), ("transpose_normed", 0), ("transpose_ctx", 1),
    ("transpose_normed", 1), ("transpose_normed", 2), ("transpose_ctx", 2), ("transpose_normed", 3), ("store", 0),
    ("transpose_ctx", 3), ("transpose_probs", 8), ("store", 1), ("transpose_probs", 9), ("store", 2),
    ("transpose_probs", 10), ("transpose_probs", 11), ("store", 3), ("transpose_probs", 12),
    ("transpose_probs", 13), ("transpose_ctx", 4),
]
POOL_ORDER = [
    ("probs_lo", 0), ("probs_lo", 1), ("residual", 0), ("probs_lo", 2), ("probs_lo", 3), ("residual", 1),
    ("probs_lo", 4), ("residual", 2), ("inverse_deviation", 0), ("probs_lo", 5), ("probs_lo", 6), ("residual", 3),
    ("probs_lo", 7),
]

AT_MOMENTS = VECTOR_ORDER.index(("mask_and_moments", 0))
VECTOR_BEFORE_MOMENTS, VECTOR_AFTER_MOMENTS = VECTOR_ORDER[:AT_MOMENTS], VECTOR_ORDER[AT_MOMENTS + 1:]

BANK_STAGES = ("project_qk", "project_v", "project_out")
BANK_USES = [use for use in TENSOR_ORDER if use[0] in BANK_STAGES]


def bank_of(stage, group, item):
    step = group - STAGES[stage][1]
    return (len(BANK_USES) * step + BANK_USES.index((stage, item))) % PROJ_BANKS


def items_of_step(order, g):
    for stage, item in order:
        count, ahead = STAGES[stage]
        group = g + ahead + item // count
        if 0 <= group < GROUPS:
            yield stage, group, item % count


def nth(per_group, group, item, i):
    return per_group * group + item + 1 + 2 * per_group * i


def loads(group, i):
    return 16 * (group // 2 + 1) + 16 * i


def transposed(g, t, i):
    return 16 * ((T * g + t) // UNITS + 1) + 16 * (2 * T // UNITS) * i


def ctx_count(g, b, i):
    return 16 * ((B * g + b) // 2 + 1) + 16 * B * i


def h_count(group, i):
    return 16 * (group + 1) + 32 * i


def projects(g):
    return 0 <= g + 1 < GROUPS


def norms(g):
    return 0 <= g + 2 < GROUPS


def build(nc, x, adj, wq, bq, wk, bk, wv, bv, wf, bf, out):
    x_v = x.rearrange("(g b) p h -> g p b h", b=B)
    adj_v = adj.rearrange("(g b) p k -> g p b k", b=B)
    out_v = out.rearrange("(g b) p h -> g p b h", b=B)

    ctx = ExitStack()
    with ctx:
        def sb(name, shape, dt=F32):
            return ctx.enter_context(nc.sbuf_tensor(name, shape, dt))

        def pb(name):
            return ctx.enter_context(nc.psum_tensor(name, [P, 512], F32))

        def sem(name):
            return ctx.enter_context(nc.semaphore(name))

        w_raw = [sb(f"w_raw{n}", [P, C, H]) for n in range(4)]
        w_hi = [sb(f"w_hi{n}", [P, C, H], F16) for n in range(4)]
        w_lo = [sb(f"w_lo{n}", [P, C, H], F16) for n in range(4)]
        w_rows_most = sb("w_rows_most", [P, 2])
        w_most = sb("w_most", [P, 4])
        w_most_all = sb("w_most_all", [P, 4])
        w_bound = sb("w_bound", [P, 4])
        w_unscale = sb("w_unscale", [P, 4])
        w_scale = sb("w_scale", [P, 4])
        score_unscale = sb("score_unscale", [P, 1])
        y_unscale = sb("y_unscale", [P, 1])
        bias_raw = sb("bias_raw", [P, 3, C])
        bias_qk = sb("bias_qk", [P, QK])
        bias_most = sb("bias_most", [P, 2])
        bv_cols = sb("bv_cols", [P, C, P])
        bf_rows = sb("bf_rows", [P, H])
        b_out = sb("b_out", [P, H])
        minus_half = sb("minus_half", [P, B])
        eps = sb("eps", [P, B])
        table_loader = sb("table_loader", [P, B])
        x_sb = [sb(f"x_sb{n}", [P, B, H]) for n in range(2)]
        x_bf = [sb(f"x_bf{n}", [P, B, H]) for n in range(2)]
        adj_sb = [sb(f"adj_sb{n}", [P, B, N], U8) for n in range(2)]
        mask = [sb(f"mask{n}", [P, B, N]) for n in range(2)]
        ht_parts = [sb(f"ht_parts{n}", [P, PARTS * C, B * N], F16) for n in range(2)]
        qkt_hi = [sb(f"qkt_hi{n}", [P, QK, B * N], F16) for n in range(2)]
        qkt_lo = [sb(f"qkt_lo{n}", [P, QK, B * N], F16) for n in range(2)]
        v_hi = [sb(f"v_hi{n}", [P, B, H], F16) for n in range(2)]
        v_lo = [sb(f"v_lo{n}", [P, B, H], F16) for n in range(2)]
        stats = sb("stats", [P, B, 6])
        moments = sb("moments", [P, B, 2])
        var_eps = sb("var_eps", [P, B])
        rstd = sb("rstd", [P, B])
        h_sb = sb("h_sb", [P, B, H])
        h_parts = [sb(f"h_parts{n}", [P, PARTS * H], F16) for n in range(B)]
        masked = [sb(f"masked{n}", [P, K, N]) for n in range(2)]
        neg_max = [sb(f"neg_max{n}", [P, K]) for n in range(2)]
        probs = [sb(f"probs{n}", [P, K, N]) for n in range(2)]
        probs_parts = [sb(f"probs_parts{n}", [P, PARTS * K * N], F16) for n in range(UNITS)]
        pt_parts = [sb(f"pt_parts{n}", [P, PARTS * K, N], F16) for n in range(UNITS)]
        sums = [sb(f"sums{n}", [P, HEADS]) for n in range(B)]
        inv_sums = [sb(f"inv_sums{n}", [P, HEADS]) for n in range(2)]
        ctx_sb = [sb(f"ctx_sb{n}", [P, H]) for n in range(2)]
        ctx_parts = [sb(f"ctx_parts{n}", [P, PARTS * H], F16) for n in range(2)]
        ct_parts = [sb(f"ct_parts{n}", [P, PARTS * C, N], F16) for n in range(2)]
        y_sb = [sb(f"y_sb{n}", [P, H]) for n in range(2)]

        ps_proj = [pb(f"ps_proj{n}") for n in range(PROJ_BANKS)]
        ps_scores = [pb(f"ps_scores{n}") for n in range(2)]
        ps_ctx = [pb(f"ps_ctx{n}") for n in range(2)]

        def proj(stage, group, item):
            return ps_proj[bank_of(stage, group, item)]

        x_loaded = [[sem(f"x_loaded{n}_{b}") for b in range(B)] for n in range(2)]
        adj_loaded = [sem(f"adj_loaded{n}") for n in range(2)]
        w_loaded = [sem(f"w_loaded{n}") for n in range(4)]
        bias_loaded = sem("bias_loaded")
        bf_loaded = sem("bf_loaded")
        probs_transposed = [sem(f"probs_transposed{n}") for n in range(UNITS)]
        h_transposed = [sem(f"h_transposed{n}") for n in range(B)]
        ctx_transposed = [sem(f"ctx_transposed{n}") for n in range(2)]
        y_stored = [sem(f"y_stored{n}") for n in range(2)]
        consts_set = sem("consts_set")
        w_reduced = sem("w_reduced")
        w_reduced_all = sem("w_reduced_all")
        row_step = sem("row_step")
        scale_step = sem("scale_step")
        unscales_ready = sem("unscales_ready")
        w_scaled = sem("w_scaled")
        w_hi_ready = sem("w_hi_ready")
        w_split = [sem(f"w_split{n}") for n in range(4)]
        biases_ready = sem("biases_ready")
        bv_ready = sem("bv_ready")
        bv_projected = sem("bv_projected")
        b_out_ready = sem("b_out_ready")
        stats_ready = sem("stats_ready")
        moments_ready = sem("moments_ready")
        var_eps_ready = sem("var_eps_ready")
        rstd_ready = sem("rstd_ready")
        h_ready = sem("h_ready")
        x_bf_ready = sem("x_bf_ready")
        mask_ready = sem("mask_ready")
        h_hi_ready = sem("h_hi_ready")
        h_split = sem("h_split")
        qk_projected = sem("qk_projected")
        qk_hi_ready = sem("qk_hi_ready")
        qk_split = sem("qk_split")
        v_projected = sem("v_projected")
        v_hi_ready = sem("v_hi_ready")
        v_split = sem("v_split")
        scores_ready = sem("scores_ready")
        scores_masked = sem("scores_masked")
        max_ready = sem("max_ready")
        probs_ready = sem("probs_ready")
        probs_hi_ready = sem("probs_hi_ready")
        probs_split = sem("probs_split")
        values_weighted = sem("values_weighted")
        sums_inverted = sem("sums_inverted")
        ctx_normalized = sem("ctx_normalized")
        ctx_hi_ready = sem("ctx_hi_ready")
        ctx_split = sem("ctx_split")
        y_projected = sem("y_projected")
        y_ready = sem("y_ready")

        sp_passed = sem("sp_passed")

        block = ctx.enter_context(nc.Block())

        @block.sync
        def _(sp):
            def store(g, b, i):
                sp.wait_ge(y_ready, nth(B, g, b, i))
                sp.dma_start(out_v[g + 2 * i, :, b, :], y_sb[b % 2][:]).then_inc(y_stored[b % 2], 16)

            def wait(semaphore, count):
                sp.wait_ge(semaphore, count)
                sp.sem_inc(sp_passed, 1)

            def transpose_probs(g, t, i):
                if g >= 1 or t >= UNITS:
                    wait(values_weighted, nth(T, g, t - UNITS, i))
                wait(probs_split, nth(T, g, t, i))
                sp.dma_start(pt_parts[t % UNITS][:], probs_parts[t % UNITS][:], transpose=True)\
                    .then_inc(probs_transposed[t % UNITS], 16)

            def transpose_ctx(g, b, i):
                if g >= 1 or b >= 2:
                    wait(y_projected, nth(B, g, b - 2, i))
                wait(ctx_split, nth(B, g, b, i))
                sp.dma_start(ct_parts[b % 2][:], ctx_parts[b % 2][:], transpose=True)\
                    .then_inc(ctx_transposed[b % 2], 16)

            def transpose_normed(group, b, i):
                if group >= 2 and b == 0:
                    wait(qk_projected, nth(QK, group - 2, QK - 1, i))
                    wait(v_projected, nth(B, group - 2, B - 1, i))
                wait(h_split, nth(B, group, b, i))
                sp.dma_start(ht_parts[group % 2][:, :, b * N:(b + 1) * N], h_parts[b][:], transpose=True)\
                    .then_inc(h_transposed[b], 16)

            stages = {"store": store, "transpose_probs": transpose_probs, "transpose_ctx": transpose_ctx,
                      "transpose_normed": transpose_normed}

            def step(g, i):
                for stage, group, item in items_of_step(SYNC_ORDER, g):
                    stages[stage](group, item, i)

            for b in range(B):
                sp.dma_start(x_sb[0][:, b, :], x_v[0, :, b, :]).then_inc(x_loaded[0][b], 16)
            for n, w in ((0, wq), (3, wf), (1, wk), (2, wv)):
                sp.dma_start(w_raw[n][:], w.rearrange("(c p) n -> p c n", p=P)).then_inc(w_loaded[n], 16)
            for b in range(B):
                transpose_normed(0, b, 0)
            step(-1, 0)
            step(0, 0)
            with sp.Fori(0, REPS) as i:
                step(1, i)
                step(2, i)
            for g in LAST:
                step(g, 0)
            for n in range(2):
                sp.wait_ge(y_stored[n], 16 * GRAPHS // 2)

        @block.gpsimd
        def _(pool):
            def inverse_deviation(group, item, i):
                pool.wait_ge(moments_ready, nth(1, group, 0, i))
                nc.gpsimd.tensor_tensor(var_eps[:], moments[:, :, 1], eps[:], ALU.add).then_inc(var_eps_ready, 1)
                pool.wait_ge(var_eps_ready, nth(1, group, 0, i))
                if group >= 1:
                    pool.wait_ge(h_ready, nth(B, group - 1, B - 1, i))
                nc.gpsimd.tensor_tensor(rstd[:], var_eps[:], minus_half[:], ALU.pow).then_inc(rstd_ready, 1)

            def residual(group, b, i):
                par = group % 2
                if group == 0 and b == 0:
                    pool.wait_ge(b_out_ready, 1)
                pool.wait_ge(x_loaded[par][b], loads(group, i))
                if group >= 2:
                    pool.wait_ge(y_ready, nth(B, group - 2, b, i))
                nc.gpsimd.tensor_tensor(x_bf[par][:, b, :], x_sb[par][:, b, :], b_out[:], ALU.add)\
                    .then_inc(x_bf_ready, 1)

            def probs_lo(g, t, i):
                pool.wait_ge(probs_hi_ready, nth(T, g, t, i))
                parts = probs_parts[t % UNITS]
                nc.gpsimd.tensor_tensor(parts[:, K * N:], probs[t % 2][:].rearrange("p k n -> p (k n)"),
                                        parts[:, 0:K * N], ALU.subtract).then_inc(probs_split, 1)

            stages = {"probs_lo": probs_lo, "inverse_deviation": inverse_deviation, "residual": residual}

            def step(g, i):
                for stage, group, item in items_of_step(POOL_ORDER, g):
                    stages[stage](group, item, i)

            def split(n):
                pool.wait_ge(w_hi_ready, n + 1)
                nc.gpsimd.tensor_tensor(w_lo[n][:], w_raw[n][:], w_hi[n][:], ALU.subtract).then_inc(w_split[n], 1)

            nc.gpsimd.memset(minus_half[:], -0.5).then_inc(consts_set, 1)
            nc.gpsimd.memset(eps[:], EPS).then_inc(consts_set, 1)
            pool.wait_ge(consts_set, 2)
            inverse_deviation(0, 0, 0)
            for n in range(4):
                pool.wait_ge(w_reduced, n + 1)
                nc.gpsimd.partition_all_reduce(w_most_all[:, n:n + 1], w_most[:, n:n + 1], P,
                                               bass.bass_isa.ReduceOp.max).then_inc(w_reduced_all, 1)
            split(2)
            step(-1, 0)
            split(3)
            step(0, 0)
            with pool.Fori(0, REPS) as i:
                step(1, i)
                step(2, i)
            for g in LAST:
                step(g, 0)

        @block.scalar
        def _(act):
            def load(group, b, i):
                par, at = group % 2, group + 2 * i
                if b == 0:
                    if group >= 2:
                        act.wait_ge(mask_ready, nth(1, group - 2, 0, i))
                    act.dma_start(adj_sb[par][:], adj_v[at, :, :, :]).then_inc(adj_loaded[par], 16)
                if group >= 2:
                    act.wait_ge(h_ready, nth(B, group - 2, b, i))
                    act.wait_ge(x_bf_ready, nth(B, group - 2, b, i))
                act.dma_start(x_sb[par][:, b, :], x_v[at, :, b, :]).then_inc(x_loaded[par][b], 16)

            def exponentials(g, t, i):
                b, half = divmod(t, HALVES)
                act.wait_ge(max_ready, nth(T, g, t, i))
                if g >= 1 or t >= 2:
                    act.wait_ge(probs_split, nth(T, g, t - 2, i))
                if g >= 1:
                    act.wait_ge(sums_inverted, nth(B, g - 1, b, i))
                for k in range(K):
                    head = HALVES * k + half
                    last = nc.scalar.activation(probs[t % 2][:, k, :], masked[t % 2][:, k, :], ACT.Exp,
                                                bias=neg_max[t % 2][:, k:k + 1],
                                                accum_out=sums[b][:, head:head + 1])
                last.then_inc(probs_ready, 1)

            def probs_hi(g, t, i):
                act.wait_ge(probs_ready, nth(T, g, t, i))
                if g >= 1 or t >= UNITS:
                    act.wait_ge(probs_transposed[t % UNITS], transposed(g, t - UNITS, i))
                nc.scalar.activation(probs_parts[t % UNITS][:, 0:K * N], probs[t % 2][:].rearrange("p k n -> p (k n)"),
                                     ACT.Copy).then_inc(probs_hi_ready, 1)

            def ctx_hi(g, b, i):
                act.wait_ge(ctx_normalized, nth(B, g, b, i))
                if g >= 1 or b >= 2:
                    act.wait_ge(ctx_transposed[b % 2], ctx_count(g, b - 2, i))
                nc.scalar.activation(ctx_parts[b % 2][:, 0:H], ctx_sb[b % 2][:], ACT.Copy).then_inc(ctx_hi_ready, 1)

            def qk_hi(group, j, i):
                act.wait_ge(qk_projected, nth(QK, group, j, i))
                if group == 0 and j % C == 0:
                    act.wait_ge(biases_ready, j // C + 1)
                if group >= 2 and j == 0:
                    act.wait_ge(scores_ready, nth(T, group - 2, T - 1, i))
                nc.scalar.activation(qkt_hi[group % 2][:, j, :], proj("project_qk", group, j)[:], ACT.Identity,
                                     bias=bias_qk[:, j:j + 1]).then_inc(qk_hi_ready, 1)

            def values_hi(group, b, i):
                act.wait_ge(v_projected, nth(B, group, b, i))
                if group >= 2 and b == 0:
                    act.wait_ge(values_weighted, nth(T, group - 2, T - 1, i))
                nc.scalar.activation(v_hi[group % 2][:, b, :], proj("project_v", group, b)[:, 0:H], ACT.Copy)\
                    .then_inc(v_hi_ready, 1)

            def normed_hi(group, b, i):
                act.wait_ge(h_ready, nth(B, group, b, i))
                if group >= 1:
                    act.wait_ge(h_transposed[b], h_count(group - 1, i))
                nc.scalar.activation(h_parts[b][:, 0:H], h_sb[:, b, :], ACT.Relu).then_inc(h_hi_ready, 1)

            stages = {"exponentials": exponentials, "probs_hi": probs_hi, "ctx_hi": ctx_hi, "qk_hi": qk_hi,
                      "values_hi": values_hi, "normed_hi": normed_hi, "load": load}

            def step(g, i):
                for stage, group, item in items_of_step(SCALAR_ORDER, g):
                    stages[stage](group, item, i)

            act.wait_ge(consts_set, 2)
            nc.scalar.activation(table_loader[:], eps[:], ACT.Exp)
            act.dma_start(bias_raw[:, 0, :], bq.rearrange("(c p) -> p c", p=P), allow_slow_non_contiguous=True)\
                .then_inc(bias_loaded, 16)
            act.dma_start(bias_raw[:, 1, :], bk.rearrange("(c p) -> p c", p=P), allow_slow_non_contiguous=True)\
                .then_inc(bias_loaded, 16)
            act.dma_start(bias_raw[:, 2, :], bv.rearrange("(c p) -> p c", p=P), allow_slow_non_contiguous=True)\
                .then_inc(bias_loaded, 16)
            act.dma_start(bf_rows[:], bf.partition_broadcast(P)).then_inc(bf_loaded, 16)
            act.dma_start(adj_sb[0][:], adj_v[0, :, :, :]).then_inc(adj_loaded[0], 16)

            def weight_hi(n):
                act.wait_ge(w_loaded[n], 16)
                act.wait_ge(scale_step, SCALE_STEPS * (n + 1))
                if n >= 2:
                    if n == 3:
                        act.wait_ge(bv_projected, 1)
                    nc.scalar.activation(w_raw[n][:], w_raw[n][:], ACT.Copy, scale=w_scale[:, n:n + 1])\
                        .then_inc(w_scaled, 1)
                    act.wait_ge(w_scaled, n - 1)
                nc.scalar.activation(w_hi[n][:], w_raw[n][:], ACT.Copy, scale=1.0 if n >= 2 else w_scale[:, n:n + 1])\
                    .then_inc(w_hi_ready, 1)

            for b in range(B):
                normed_hi(0, b, 0)
            weight_hi(0)
            for b in range(B):
                load(1, b, 0)
            for n in range(1, 4):
                weight_hi(n)
            step(-1, 0)
            step(0, 0)
            with act.Fori(0, REPS) as i:
                step(1, i)
                step(2, i)
            for g in LAST:
                step(g, 0)

        @block.vector
        def _(dve):
            def statistics(group, b, i):
                dve.wait_ge(x_loaded[group % 2][b], loads(group, i))
                if group >= 1 and b == 0:
                    dve.wait_ge(moments_ready, nth(1, group - 1, 0, i))
                nc.vector.bn_stats(stats[:, b, :], x_sb[group % 2][:, b, :]).then_inc(stats_ready, 1)

            def additive_mask(group, i):
                dve.wait_ge(adj_loaded[group % 2], loads(group, i))
                if group >= 2:
                    dve.wait_ge(scores_masked, nth(T, group - 2, T - 1, i))
                nc.vector.tensor_scalar(mask[group % 2][:], adj_sb[group % 2][:], -NEG, NEG, ALU.mult, ALU.add)\
                    .then_inc(mask_ready, 1)

            def wait_to_aggregate(group, i):
                dve.wait_ge(stats_ready, nth(B, group, B - 1, i))
                if group >= 1:
                    dve.wait_ge(h_ready, nth(B, group - 1, B - 1, i))
                    dve.wait_ge(var_eps_ready, nth(1, group - 1, 0, i))

            def aggregate(group):
                for b in range(B):
                    last = nc.vector.bn_aggr(moments[:, b, :], stats[:, b, :])
                last.then_inc(moments_ready, 1)

            def normalize(group, b, i):
                dve.wait_ge(rstd_ready, nth(1, group, 0, i))
                if group >= 1:
                    dve.wait_ge(h_split, nth(B, group - 1, b, i))
                nc.vector.tensor_scalar(h_sb[:, b, :], x_sb[group % 2][:, b, :], moments[:, b, 0:1],
                                        rstd[:, b:b + 1], ALU.subtract, ALU.mult).then_inc(h_ready, 1)

            def mask_and_max(g, t, i):
                dve.wait_ge(scores_ready, nth(T, g, t, i))
                dve.wait_ge(mask_ready, nth(1, g, 0, i))
                if g >= 1 or t >= 2:
                    dve.wait_ge(probs_ready, nth(T, g, t - 2, i))
                nc.vector.scalar_tensor_tensor(
                    out=masked[t % 2][:], in0=ps_scores[t % 2][:, 0:K * N].rearrange("p (k n) -> p k n", k=K),
                    scalar=score_unscale[:, 0:1],
                    in1=mask[g % 2][:, t // HALVES, :].unsqueeze(1).broadcast_to([P, K, N]),
                    op0=ALU.mult, op1=ALU.add).then_inc(scores_masked, 1)
                dve.wait_ge(scores_masked, nth(T, g, t, i))
                nc.vector.tensor_reduce(neg_max[t % 2][:], masked[t % 2][:], AX.X, ALU.max, negate=True)\
                    .then_inc(max_ready, 1)

            def normalize_ctx(g, b, i):
                dve.wait_ge(probs_ready, nth(T, g, HALVES * b + 1, i))
                if g >= 1 or b >= 2:
                    dve.wait_ge(ctx_normalized, nth(B, g, b - 2, i))
                nc.vector.reciprocal(inv_sums[b % 2][:], sums[b][:]).then_inc(sums_inverted, 1)
                dve.wait_ge(sums_inverted, nth(B, g, b, i))
                dve.wait_ge(values_weighted, nth(T, g, HALVES * b + 1, i))
                if g >= 1 or b >= 2:
                    dve.wait_ge(ctx_split, nth(B, g, b - 2, i))
                nc.vector.tensor_tensor(ctx_sb[b % 2][:].rearrange("p (h d) -> p h d", h=HEADS),
                                        ps_ctx[b % 2][:, 0:H].rearrange("p (h d) -> p h d", h=HEADS),
                                        inv_sums[b % 2][:].unsqueeze(2).broadcast_to([P, HEADS, D]),
                                        ALU.mult).then_inc(ctx_normalized, 1)

            def ctx_lo(g, b, i):
                dve.wait_ge(ctx_hi_ready, nth(B, g, b, i))
                parts = ctx_parts[b % 2]
                nc.vector.tensor_tensor(parts[:, H:], ctx_sb[b % 2][:], parts[:, 0:H], ALU.subtract)\
                    .then_inc(ctx_split, 1)

            def finish(g, b, i):
                dve.wait_ge(y_projected, nth(B, g, b, i))
                dve.wait_ge(x_bf_ready, nth(B, g, b, i))
                if g >= 1 or b >= 2:
                    dve.wait_ge(y_stored[b % 2], 16 * (2 * g + b // 2) + 64 * i)
                nc.vector.scalar_tensor_tensor(out=y_sb[b % 2][:], in0=proj("project_out", g, b)[:, 0:H],
                                               scalar=y_unscale[:, 0:1], in1=x_bf[g % 2][:, b, :],
                                               op0=ALU.mult, op1=ALU.add).then_inc(y_ready, 1)

            def qk_lo(group, j, i):
                dve.wait_ge(qk_hi_ready, nth(QK, group, j, i))
                nc.vector.scalar_tensor_tensor(out=qkt_lo[group % 2][:, j, :], in0=proj("project_qk", group, j)[:],
                                               scalar=bias_qk[:, j:j + 1], in1=qkt_hi[group % 2][:, j, :],
                                               op0=ALU.add, op1=ALU.subtract).then_inc(qk_split, 1)

            def values_lo(group, b, i):
                dve.wait_ge(v_hi_ready, nth(B, group, b, i))
                nc.vector.tensor_tensor(v_lo[group % 2][:, b, :], proj("project_v", group, b)[:, 0:H],
                                        v_hi[group % 2][:, b, :], ALU.subtract).then_inc(v_split, 1)

            def normed_lo(group, b, i):
                dve.wait_ge(h_hi_ready, nth(B, group, b, i))
                parts = h_parts[b]
                nc.vector.scalar_tensor_tensor(out=parts[:, H:], in0=h_sb[:, b, :], scalar=0.0, in1=parts[:, 0:H],
                                               op0=ALU.max, op1=ALU.subtract).then_inc(h_split, 1)

            def mask_and_moments(g, i):
                if norms(g):
                    wait_to_aggregate(g + 2, i)
                if projects(g):
                    additive_mask(g + 1, i)
                if norms(g):
                    aggregate(g + 2)

            stages = {"mask_and_max": mask_and_max, "qk_lo": qk_lo, "normalize_ctx": normalize_ctx,
                      "ctx_lo": ctx_lo, "finish": finish, "values_lo": values_lo, "statistics": statistics,
                      "normalize": normalize, "normed_lo": normed_lo}

            def step(g, i):
                for stage, group, item in items_of_step(VECTOR_BEFORE_MOMENTS, g):
                    stages[stage](group, item, i)
                mask_and_moments(g, i)
                for stage, group, item in items_of_step(VECTOR_AFTER_MOMENTS, g):
                    stages[stage](group, item, i)

            def largest(n):
                dve.wait_ge(w_loaded[n], 16)
                if n >= 2:
                    nc.vector.tensor_reduce(w_most[:, n:n + 1], w_raw[n][:], AX.XY, ALU.max,
                                            apply_absolute_value=True).then_inc(w_reduced, 1)
                    return
                nc.vector.tensor_reduce(w_rows_most[:, n:n + 1], w_raw[n][:], AX.XY, ALU.max,
                                        apply_absolute_value=True).then_inc(row_step, 1)
                dve.wait_ge(row_step, n + 2)
                nc.vector.tensor_tensor(w_most[:, n:n + 1], w_rows_most[:, n:n + 1], bias_most[:, n:n + 1], ALU.max)\
                    .then_inc(w_reduced, 1)

            def scale(n):
                at, before = slice(n, n + 1), SCALE_STEPS * n
                dve.wait_ge(w_reduced_all, n + 1)
                nc.vector.tensor_scalar(w_bound[:, at], w_most_all[:, at], TINY, 1.0 / WEIGHT_MOST, ALU.max, ALU.mult)\
                    .then_inc(scale_step, 1)
                dve.wait_ge(scale_step, before + 1)
                nc.vector.tensor_scalar(w_unscale[:, at].bitcast(I32), w_bound[:, at].bitcast(I32), EXPONENT_BITS,
                                        None, ALU.bitwise_and).then_inc(scale_step, 1)
                dve.wait_ge(scale_step, before + 2)
                nc.vector.reciprocal(w_scale[:, at], w_unscale[:, at]).then_inc(scale_step, 1)

            def scale_bias(n):
                dve.wait_ge(scale_step, SCALE_STEPS * (n + 1))
                nc.vector.tensor_scalar(bias_qk[:, n * C:(n + 1) * C], bias_raw[:, n, :], w_scale[:, n:n + 1], None,
                                        ALU.mult).then_inc(biases_ready, 1)

            def split(n):
                dve.wait_ge(w_hi_ready, n + 1)
                nc.vector.scalar_tensor_tensor(out=w_lo[n][:], in0=w_raw[n][:], scalar=w_scale[:, n:n + 1],
                                               in1=w_hi[n][:], op0=ALU.mult, op1=ALU.subtract).then_inc(w_split[n], 1)

            for b in range(B):
                statistics(0, b, 0)
            mask_and_moments(-2, 0)
            dve.wait_ge(bias_loaded, 48)
            nc.vector.tensor_reduce(bias_most[:], bias_raw[:, 0:2, :], AX.X, ALU.max, apply_absolute_value=True)\
                .then_inc(row_step, 1)
            nc.vector.tensor_copy(bv_cols[:], bias_raw[:, 2, :].unsqueeze(2).broadcast_to([P, C, P]))\
                .then_inc(bv_ready, 1)
            for b in range(B):
                normalize(0, b, 0)
            normed_lo(0, 0, 0)
            normed_lo(0, 1, 0)
            largest(0)
            normed_lo(0, 2, 0)
            normed_lo(0, 3, 0)
            scale(0)
            largest(1)
            split(0)
            scale_bias(0)
            scale(1)
            largest(2)
            split(1)
            scale_bias(1)
            scale(2)
            dve.wait_ge(bv_projected, 1)
            dve.wait_ge(bf_loaded, 16)
            nc.vector.tensor_tensor(b_out[:], ps_ctx[0][:, 0:H], bf_rows[:], ALU.add).then_inc(b_out_ready, 1)
            largest(3)
            nc.vector.tensor_scalar(score_unscale[:], w_unscale[:, 0:1], w_unscale[:, 1:2], SCALE, ALU.mult, ALU.mult)\
                .then_inc(unscales_ready, 1)
            scale(3)
            dve.wait_ge(scale_step, 4 * SCALE_STEPS)
            nc.vector.tensor_tensor(y_unscale[:], w_unscale[:, 2:3], w_unscale[:, 3:4], ALU.mult)\
                .then_inc(unscales_ready, 1)
            dve.wait_ge(unscales_ready, 2)
            step(-1, 0)
            step(0, 0)
            with dve.Fori(0, REPS) as i:
                step(1, i)
                step(2, i)
            for g in LAST:
                step(g, 0)

        @block.tensor
        def _(pe):
            last_use = {}

            def wait_for_bank(kind, j, group, i):
                bank = bank_of(kind, group, j)
                if bank in last_use:
                    was, item, of = last_use[bank]
                    if was == "project_qk":
                        pe.wait_ge(qk_split, nth(QK, of, item, i))
                    if was == "project_v":
                        pe.wait_ge(v_split, nth(B, of, item, i))
                    if was == "project_out":
                        pe.wait_ge(y_ready, nth(B, of, item, i))
                last_use[bank] = kind, j, group
                return ps_proj[bank]

            def three_passes(out, a_hi, a_lo, b_hi, b_lo, first, last):
                nc.tensor.matmul(out, a_hi, b_hi, start=first, stop=False)
                nc.tensor.matmul(out, a_hi, b_lo, start=False, stop=False)
                return nc.tensor.matmul(out, a_lo, b_hi, start=False, stop=last)

            def project_qk(group, j, i):
                w, m = divmod(j, C)
                if j == 0:
                    for b in range(B):
                        pe.wait_ge(h_transposed[b], h_count(group, i))
                if group == 0 and m == 0:
                    pe.wait_ge(w_split[w], 1)
                ps = wait_for_bank("project_qk", j, group, i)
                hi, lo = ht_parts[group % 2][:, 0:C, :], ht_parts[group % 2][:, C:, :]
                at = slice(m * P, (m + 1) * P)
                for c in range(C):
                    last = three_passes(ps[:], w_hi[w][:, c, at], w_lo[w][:, c, at], hi[:, c, :], lo[:, c, :],
                                        c == 0, c == C - 1)
                last.then_inc(qk_projected, 1)

            def project_v(group, b, i):
                if group == 0 and b == 0:
                    pe.wait_ge(w_split[2], 1)
                ps = wait_for_bank("project_v", b, group, i)
                hi, lo = ht_parts[group % 2][:, 0:C, :], ht_parts[group % 2][:, C:, :]
                at = slice(b * N, (b + 1) * N)
                for c in range(C):
                    last = three_passes(ps[:, 0:H], hi[:, c, at], lo[:, c, at], w_hi[2][:, c, :], w_lo[2][:, c, :],
                                        c == 0, c == C - 1)
                last.then_inc(v_projected, 1)

            def scores(g, t, i):
                b, half = divmod(t, HALVES)
                if t == 0:
                    pe.wait_ge(qk_split, nth(QK, g, QK - 1, i))
                if g >= 1 or t >= 2:
                    pe.wait_ge(scores_masked, nth(T, g, t - 2, i))
                hi, lo = qkt_hi[g % 2], qkt_lo[g % 2]
                rows, at = slice(half * D, (half + 1) * D), slice(b * N, (b + 1) * N)
                for k in range(K):
                    last = three_passes(ps_scores[t % 2][:, k * N:(k + 1) * N], hi[rows, k, at], lo[rows, k, at],
                                        hi[rows, C + k, at], lo[rows, C + k, at], True, True)
                last.then_inc(scores_ready, 1)

            def weigh_values(g, t, i):
                b, half = divmod(t, HALVES)
                pe.wait_ge(probs_transposed[t % UNITS], transposed(g, t, i))
                if t == 0:
                    pe.wait_ge(v_split, nth(B, g, B - 1, i))
                if g == 0 and t == 0:
                    pe.wait_ge(b_out_ready, 1)
                if half == 0 and (g >= 1 or b >= 2):
                    pe.wait_ge(ctx_normalized, nth(B, g, b - 2, i))
                hi, lo = pt_parts[t % UNITS][:, 0:K, :], pt_parts[t % UNITS][:, K:, :]
                for k in range(K):
                    head = HALVES * k + half
                    at = slice(head * D, (head + 1) * D)
                    last = three_passes(ps_ctx[b % 2][:, at], hi[:, k, :], lo[:, k, :],
                                        v_hi[g % 2][:, b, at], v_lo[g % 2][:, b, at], True, True)
                last.then_inc(values_weighted, 1)

            def project_out(g, b, i):
                pe.wait_ge(ctx_transposed[b % 2], ctx_count(g, b, i))
                if g == 0 and b == 0:
                    pe.wait_ge(w_split[3], 1)
                ps = wait_for_bank("project_out", b, g, i)
                for c in range(C):
                    last = three_passes(ps[:, 0:H], ct_parts[b % 2][:, c, :], ct_parts[b % 2][:, C + c, :],
                                        w_hi[3][:, c, :], w_lo[3][:, c, :], c == 0, c == C - 1)
                last.then_inc(y_projected, 1)

            stages = {"scores": scores, "weigh_values": weigh_values,
                      "project_out": project_out, "project_qk": project_qk, "project_v": project_v}

            def step(g, i):
                for stage, group, item in items_of_step(TENSOR_ORDER, g):
                    stages[stage](group, item, i)

            pe.wait_ge(bv_ready, 1)
            pe.wait_ge(w_loaded[3], 16)
            for c in range(C):
                last = nc.tensor.matmul(ps_ctx[0][:, 0:H], bv_cols[:, c, :], w_raw[3][:, c, :],
                                        start=c == 0, stop=c == C - 1)
            last.then_inc(bv_projected, 1)
            step(-1, 0)
            step(0, 0)
            with pe.Fori(0, REPS) as i:
                step(1, i)
                step(2, i)
            for bank, (kind, j, group) in last_use.items():
                last_use[bank] = kind, j, group + 2 * (REPS - 1)
            for g in LAST:
                step(g, 0)


_INS = ["x", "adj", "L0_gnn_Wq", "L0_gnn_bq", "L0_gnn_Wk", "L0_gnn_bk", "L0_gnn_Wv", "L0_gnn_bv", "L0_gnn_Wf",
        "L0_gnn_bf"]


def kernel(**inputs):
    import numpy as _np
    import concourse.bacc as _bacc
    from concourse import mybir as _mybir
    from concourse.bass_utils import run_bass_kernel_spmd as _run

    nc = _bacc.Bacc("TRN2", target_bir_lowering=False, num_devices=1)
    arrays, args = {}, []
    for name in _INS:
        a = _np.ascontiguousarray(inputs[name])
        arrays[f"in_{name}"] = a
        args.append(nc.dram_tensor(f"in_{name}", a.shape, _mybir.dt.from_np(a.dtype), kind="ExternalInput").ap())
    y = nc.dram_tensor("y", (GRAPHS, N, H), _mybir.dt.float32, kind="ExternalOutput").ap()
    build(nc, *args, y)
    r = _run(nc, [arrays], core_ids=[0])
    return r.results[0]["y"]
```
